# Optimizing a Trainium2 kernel written in Bass

```python
import numpy as np
import jax
import jax.numpy as jnp

def _softmax(x, axis=-1):
    return jax.nn.softmax(x, axis=axis)
def _gelu(x):
    return jax.nn.gelu(x, approximate=True)
def _silu(x):
    return jax.nn.silu(x)
def _sigmoid(x):
    return jax.nn.sigmoid(x)
def _layernorm(x, axis=-1, eps=1e-5):
    m = jnp.mean(x, axis=axis, keepdims=True)
    v = jnp.var(x, axis=axis, keepdims=True)
    return (x - m) / jnp.sqrt(v + eps)
def _scatter_add(tgt, idx, src, axis=0):
    return tgt.at[idx].add(src)
def _segment_sum(src, seg, n):
    return jax.ops.segment_sum(src, seg, n)

kernel_name = 'mk_adj_resnorm_d1_adj_512_1c831e'

def setup_inputs(seed: int = 0):
    np.random.seed(seed)
    _w = jnp.asarray
    def _rec_inputs():
        import jax
        import jax.numpy as jnp
        _gk = jax.random.key(seed)
        x = -0.0005963 + 1.001 * jax.random.normal(jax.random.fold_in(_gk, 1), (6144, 512), jnp.float32)
        _a = jax.random.bernoulli(jax.random.fold_in(_gk, 2), 0.00520833, (6144, 6144))
        _a = jnp.logical_or(_a, jnp.swapaxes(_a, -1, -2))
        _a = jnp.logical_or(_a, jnp.eye(6144, dtype=bool))
        adj = _a.astype(jnp.int32)
        return x, adj
    x, adj = _rec_inputs()
    def _L0_gnn_setup():
        import jax, jax.numpy as jnp
        import numpy as np
        N = 6144
        IN_FEATS = 512
        OUT_FEATS = 64
        NHEADS = 8
        ALPHA = 0.2
        NEG_BIG = -9000000000000000.0
        key = jax.random.key(seed)
        k_x, k_adj, k_w, k_a1, k_a2 = jax.random.split(key, 5)
        x = jax.random.normal(k_x, (N, IN_FEATS), dtype=jnp.float32)
        adj = jax.random.randint(k_adj, (N, N), 0, 2, dtype=jnp.int32)
        gain = 1.414
        bw = gain * np.sqrt(6.0 / (IN_FEATS + OUT_FEATS))
        W = jax.random.uniform(k_w, (NHEADS, IN_FEATS, OUT_FEATS), jnp.float32, -bw, bw)
        ba = gain * np.sqrt(6.0 / (OUT_FEATS + 1))
        a1 = jax.random.uniform(k_a1, (NHEADS, OUT_FEATS), jnp.float32, -ba, ba)
        a2 = jax.random.uniform(k_a2, (NHEADS, OUT_FEATS), jnp.float32, -ba, ba)
        return {'x': x, 'adj': adj, 'W': W, 'a1': a1, 'a2': a2}
    _L0_gnn_all = _L0_gnn_setup()
    _L0_gnn_in = {k: v for k, v in _L0_gnn_all.items() if k in ('W', 'a1', 'a2', )}
    del _L0_gnn_all

    return {
        "x": x,
        "adj": adj,
        "L0_gnn_W": _L0_gnn_in["W"],
        "L0_gnn_a1": _L0_gnn_in["a1"],
        "L0_gnn_a2": _L0_gnn_in["a2"],
    }

def reference(x, adj, L0_gnn_W, L0_gnn_a1, L0_gnn_a2):
    import jax
    import jax.numpy as jnp
    def _L0_gnn_ref(x, adj, W, a1, a2):
        import jax, jax.numpy as jnp
        import numpy as np
        N = 6144
        IN_FEATS = 512
        OUT_FEATS = 64
        NHEADS = 8
        ALPHA = 0.2
        NEG_BIG = -9000000000000000.0
        h = jnp.einsum('ni,hif->hnf', x, W)
        s1 = jnp.einsum('hnf,hf->hn', h, a1)
        s2 = jnp.einsum('hnf,hf->hn', h, a2)
        scores = jax.nn.leaky_relu(s1[:, :, None] + s2[:, None, :], negative_slope=ALPHA)
        scores = jnp.where(adj[None] > 0, scores, NEG_BIG)
        att = jax.nn.softmax(scores, axis=-1)
        out = jnp.einsum('hnm,hmf->hnf', att, h)
        out = jnp.transpose(out, (1, 0, 2)).reshape(N, NHEADS * OUT_FEATS)
        return jax.nn.elu(out)

    x = _layernorm(x + _L0_gnn_ref(x, adj, L0_gnn_W, L0_gnn_a1, L0_gnn_a2), axis=-1)
    return x


_drawn_inputs = setup_inputs


def setup_inputs(seed=0):
    import zlib

    import numpy as np

    out = dict(_drawn_inputs(seed))
    spreads = {}
    factors = {}
    for name, (base, spread) in spreads.items():
        noise = np.random.default_rng([zlib.crc32(name.encode()), seed]).standard_normal(out[name].shape)
        drawn = base * np.exp(spread * noise) if base else spread * noise
        out[name] = jnp.asarray(drawn.astype(out[name].dtype))
    for name, factor in factors.items():
        out[name] = (out[name] * factor).astype(out[name].dtype)
    return out
```

```python
def build(nc, x, x_t, adj, adj_t, w, a1, a2, out):
    from contextlib import ExitStack

    import concourse.bass as bass
    from concourse import mybir

    f32, f16, i32 = mybir.dt.float32, mybir.dt.float16, mybir.dt.int32
    ALU = mybir.AluOpType
    ACT = mybir.ActivationFunctionType
    AX = mybir.AxisListType
    RMAX = bass.bass_isa.ReduceOp.max
    ds = bass.ds

    P = 128
    N, D = x.shape
    H = a1.shape[0]
    F = a1.shape[1]
    KT = D // P
    MT = N // P
    CHUNK = 512
    CHUNKS = N // CHUNK
    TPC = CHUNK // P
    SLOPE = 0.2
    NEG_BIG = 9.0e15
    EPS = 1e-5

    h_dram = nc.dram_tensor("h_scratch", [MT, P, D], f32, kind="Internal").ap()
    s_rows_dram = nc.dram_tensor("s_rows_scratch", [2 * H, N], f32, kind="Internal").ap()

    keep = ExitStack()
    with keep:
        def sem(name):
            return keep.enter_context(nc.semaphore(name))

        s_col = keep.enter_context(nc.sbuf_tensor("s_col", [P, MT, 2 * H], f32))
        ident = keep.enter_context(nc.sbuf_tensor("ident", [P, P], f32))

        with ExitStack() as ph:
            def sb(name, shape, dt):
                return ph.enter_context(nc.sbuf_tensor(name, shape, dt))

            w_sb = sb("w_sb", [P, KT, D], f32)
            a_b = sb("a_b", [P, 2, D], f32)
            wa_prod = sb("wa_prod", [P, 2, D], f32)
            wa = sb("wa", [P, KT, 2 * H], f32)
            xt_sb = sb("xt_sb", [P, KT, N], f32)
            h_sb = sb("h_sb", [P, 2, D], f32)
            s_t = sb("s_t", [2 * H, N], f32)
            ps_s = ph.enter_context(nc.psum_tensor("ps_s", [P, 1024], f32))
            ps_t = ph.enter_context(nc.psum_tensor("ps_t", [P, 2, CHUNK], f32))
            ps_h = ph.enter_context(nc.psum_tensor("ps_h", [P, 4, D], f32))

            w_loaded, a_loaded, x_loaded = sem("w_loaded"), sem("a_loaded"), [sem(f"x_loaded{c}") for c in range(CHUNKS)]
            id_zero, id_ready = sem("id_zero"), sem("id_ready")
            wa_prod_done, wa_ready = sem("wa_prod_done"), sem("wa_ready")
            s_done, s_col_ready = sem("s_done"), sem("s_col_ready")
            st_done, st_ready = sem("st_done"), sem("st_ready")
            h_done, h_copied, rows_stored = sem("h_done"), sem("h_copied"), sem("rows_stored")
            h_stored = [sem("h_stored0"), sem("h_stored1")]

            block = ph.enter_context(nc.Block())

            @block.sync
            def _(sp):
                sp.dma_start(w_sb[:], w.rearrange("(t p) c -> p t c", p=P)).then_inc(w_loaded, 16)
                for a, src in enumerate((a1, a2)):
                    flat = src.rearrange("h f -> (h f)")[None, :]
                    sp.dma_start(a_b[:, a, :], flat.broadcast_to([P, D])).then_inc(a_loaded, 16)
                for c in range(CHUNKS):
                    part = x_t[:, c * CHUNK:(c + 1) * CHUNK].rearrange("(t p) n -> p t n", p=P)
                    sp.dma_start(xt_sb[:, :, c * CHUNK:(c + 1) * CHUNK], part).then_inc(x_loaded[c], 16)
                sp.wait_ge(st_ready, CHUNKS)
                sp.dma_start(s_rows_dram, s_t[:]).then_inc(rows_stored, 16)
                for m in range(MT):
                    sp.wait_ge(h_copied, m + 1)
                    sp.dma_start(h_dram[m], h_sb[:, m % 2, :]).then_inc(h_stored[m % 2], 16)
                for slot in range(2):
                    sp.wait_ge(h_stored[slot], 16 * MT // 2)
                sp.wait_ge(rows_stored, 16)

            @block.gpsimd
            def _(pool):
                nc.gpsimd.memset(ident[:], 0.0).then_inc(id_zero, 1)
                pool.wait_ge(id_zero, 1)
                nc.gpsimd.affine_select(out=ident[:], in_=ident[:], compare_op=ALU.not_equal, fill=1.0, base=0,
                                        pattern=[[-1, P]], channel_multiplier=1).then_inc(id_ready, 1)

            @block.vector
            def _(dve):
                dve.wait_ge(w_loaded, 16)
                dve.wait_ge(a_loaded, 32)
                for n in range(2 * KT):
                    a, k = n % 2, n // 2
                    if n >= 2:
                        dve.wait_ge(wa_ready, n - 1)
                    nc.vector.tensor_tensor(wa_prod[:, n % 2, :], w_sb[:, k, :], a_b[:, a, :],
                                            ALU.mult).then_inc(wa_prod_done, 1)
                    dve.wait_ge(wa_prod_done, n + 1)
                    nc.vector.tensor_reduce(wa[:, k, a * H:(a + 1) * H],
                                            wa_prod[:, n % 2, :].rearrange("p (h f) -> p h f", f=F),
                                            axis=AX.X, op=ALU.add).then_inc(wa_ready, 1)
                dve.wait_ge(s_done, MT)
                nc.vector.tensor_copy(s_col[:].rearrange("p m s -> p (m s)"),
                                      ps_s[:, 0:MT * 2 * H]).then_inc(s_col_ready, 1)

            @block.tensor
            def _(pe):
                pe.wait_ge(wa_ready, 2 * KT)
                for m in range(MT):
                    if m % TPC == 0:
                        pe.wait_ge(x_loaded[m // TPC], 16)
                    for k in range(KT):
                        last = nc.tensor.matmul(ps_s[:, m * 2 * H:(m + 1) * 2 * H], xt_sb[:, k, m * P:(m + 1) * P],
                                                wa[:, k, :], start=k == 0, stop=k == KT - 1)
                    last.then_inc(s_done, 1)
                pe.wait_ge(id_ready, 1)
                pe.wait_ge(s_col_ready, 1)
                for c in range(CHUNKS):
                    if c >= 2:
                        pe.wait_ge(st_ready, c - 1)
                    for t in range(TPC):
                        last = nc.tensor.transpose(ps_t[0:2 * H, c % 2, t * P:(t + 1) * P],
                                                   s_col[:, c * TPC + t, :], ident[:])
                    last.then_inc(st_done, 1)
                for m in range(MT):
                    if m >= 4:
                        pe.wait_ge(h_copied, m - 3)
                    for k in range(KT):
                        last = nc.tensor.matmul(ps_h[:, m % 4, :], xt_sb[:, k, m * P:(m + 1) * P], w_sb[:, k, :],
                                                start=k == 0, stop=k == KT - 1)
                    last.then_inc(h_done, 1)

            @block.scalar
            def _(act):
                for c in range(CHUNKS):
                    act.wait_ge(st_done, c + 1)
                    nc.scalar.copy(s_t[:, c * CHUNK:(c + 1) * CHUNK], ps_t[0:2 * H, c % 2, :]).then_inc(st_ready, 1)
                for m in range(MT):
                    act.wait_ge(h_done, m + 1)
                    if m >= 2:
                        act.wait_ge(h_stored[m % 2], 16 * (m // 2))
                    nc.scalar.copy(h_sb[:, m % 2, :], ps_h[:, m % 4, :]).then_inc(h_copied, 1)

        with ExitStack() as ph:
            def sb(name, shape, dt):
                return ph.enter_context(nc.sbuf_tensor(name, shape, dt))

            adj_row = sb("adj_row", [P, N], i32)
            mask = sb("mask", [P, N], f32)
            s2_b = sb("s2_b", [P, N], f32)
            score = sb("score", [P, N], f32)
            e_t = sb("e_t", [P, MT, P], f32)
            h_head = sb("h_head", [P, MT, F], f32)
            x_row = sb("x_row", [P, D], f32)
            att = sb("att", [P, D], f32)
            elu_n = sb("elu_n", [P, D], f32)
            y_row = sb("y_row", [P, D], f32)
            neg_max = sb("neg_max", [P, 1], f32)
            den = sb("den", [P, 1], f32)
            rden = sb("rden", [P, 1], f32)
            stats = sb("stats", [P, 6], f32)
            mv = sb("mv", [P, 2], f32)
            rstd = sb("rstd", [P, 1], f32)
            expo = sb("expo", [P, 1], f32)
            neg_off = adj_row[:].bitcast(f32)
            scaled = e_t[:].rearrange("p m n -> p (m n)")
            ps_e = ph.enter_context(nc.psum_tensor("ps_e", [P, 2, 4 * P], f32))
            ps_o = ph.enter_context(nc.psum_tensor("ps_o", [P, 512], f32))
            TG = MT // 4

            g_adj, g_x, g_s2, g_h = sem("g_adj"), sem("g_x"), sem("g_s2"), sem("g_h")
            g_mask, g_off = sem("g_mask"), sem("g_off")
            g_dve, g_exp, g_tr, g_trc, g_pv = sem("g_dve"), sem("g_exp"), sem("g_tr"), sem("g_trc"), sem("g_pv")
            g_tail, g_elu, g_pow, g_y, g_out = sem("g_tail"), sem("g_elu"), sem("g_pow"), sem("g_y"), sem("g_out")
            g_ex, g_free = sem("g_ex"), sem("g_free")
            block = ph.enter_context(nc.Block())
            STEPS = 5
            TAIL = 6

            @block.sync
            def _(sp):
                sp.sem_inc(g_free, 1)
                sp.sem_inc(g_out, 16)
                with sp.Fori(0, MT) as i:
                    sp.dma_start(adj_row[:], adj[ds(i * P, P), :]).then_inc(g_adj, 16)
                    sp.dma_start(x_row[:], x[ds(i * P, P), :]).then_inc(g_x, 16)
                    with sp.Fori(0, H) as h:
                        sp.wait_ge(g_free, i * H + h + 1)
                        sp.dma_start(s2_b[:], s_rows_dram[ds(h + H, 1), :].broadcast_to([P, N])).then_inc(g_s2, 16)
                        sp.dma_start(h_head[:], h_dram.rearrange("m p (h f) -> h p m f", f=F)[ds(h, 1)]
                                     .rearrange("a p m f -> (a p) m f")).then_inc(g_h, 16)
                    sp.wait_ge(g_y, i + 1)
                    sp.dma_start(out[ds(i * P, P), :], y_row[:]).then_inc(g_out, 16)
                sp.wait_ge(g_out, 16 * MT + 16)

            @block.vector
            def _(dve):
                with dve.Fori(0, MT) as i:
                    dve.wait_ge(g_adj, i * 16 + 16)
                    nc.vector.tensor_scalar(mask[:], adj_row[:], 0.0, None, ALU.is_gt).then_inc(g_mask, 1)
                    dve.wait_ge(g_mask, i + 1)
                    nc.vector.tensor_scalar(neg_off, mask[:], -1.0, NEG_BIG, ALU.add, ALU.mult).then_inc(g_off, 1)
                    with dve.Fori(0, H) as h:
                        n = dve.snap(i * H + h)
                        base = dve.snap(n * STEPS)
                        s1 = s_col[:, ds(i, 1), ds(h, 1)].rearrange("p a b -> p (a b)")
                        dve.wait_ge(g_s2, n * 16 + 16)
                        nc.vector.tensor_scalar(scaled, s2_b[:], s1, SLOPE, ALU.add, ALU.mult).then_inc(g_dve, 1)
                        dve.wait_ge(g_dve, base + 1)
                        nc.vector.scalar_tensor_tensor(out=score[:], in0=s2_b[:], scalar=s1, in1=scaled,
                                                       op0=ALU.add, op1=ALU.max).then_inc(g_dve, 1)
                        dve.wait_ge(g_dve, base + 2)
                        nc.vector.tensor_tensor(score[:], score[:], mask[:], ALU.mult).then_inc(g_dve, 1)
                        dve.wait_ge(g_off, i + 1)
                        dve.wait_ge(g_dve, base + 3)
                        nc.vector.tensor_tensor(score[:], score[:], neg_off, ALU.add).then_inc(g_dve, 1)
                        dve.wait_ge(g_dve, base + 4)
                        nc.vector.tensor_reduce(neg_max[:], score[:], axis=AX.X, op=ALU.max, negate=True).then_inc(g_dve, 1)
                        dve.wait_ge(g_exp, n + 1)
                        nc.vector.reciprocal(rden[:], den[:]).then_inc(g_ex, 1)
                        dve.wait_ge(g_ex, n + 1)
                        dve.wait_ge(g_pv, n + 1)
                        nc.vector.tensor_scalar(att[:, ds(h * F, F)], ps_o[:, 0:F], rden[:], None,
                                                ALU.mult).then_inc(g_free, 1)
                    tail = dve.snap(i * TAIL)
                    dve.wait_ge(g_free, i * H + H + 1)
                    nc.vector.tensor_scalar_min(elu_n[:], att[:], 0.0).then_inc(g_tail, 1)
                    dve.wait_ge(g_elu, i + 1)
                    dve.wait_ge(g_x, i * 16 + 16)
                    nc.vector.scalar_tensor_tensor(out=elu_n[:], in0=elu_n[:], scalar=-1.0, in1=x_row[:],
                                                   op0=ALU.add, op1=ALU.add).then_inc(g_tail, 1)
                    dve.wait_ge(g_tail, tail + 2)
                    nc.vector.scalar_tensor_tensor(out=att[:], in0=att[:], scalar=0.0, in1=elu_n[:],
                                                   op0=ALU.max, op1=ALU.add).then_inc(g_tail, 1)
                    dve.wait_ge(g_tail, tail + 3)
                    nc.vector.bn_stats(stats[:], att[:]).then_inc(g_tail, 1)
                    dve.drain()
                    nc.vector.bn_aggr(mv[:], stats[:]).then_inc(g_tail, 1)
                    dve.wait_ge(g_tail, tail + 5)
                    nc.vector.tensor_scalar_add(mv[:, 1:2], mv[:, 1:2], EPS).then_inc(g_tail, 1)
                    dve.wait_ge(g_out, i * 16 + 16)
                    dve.wait_ge(g_pow, i + 2)
                    nc.vector.tensor_scalar(y_row[:], att[:], mv[:, 0:1], rstd[:], ALU.subtract,
                                            ALU.mult).then_inc(g_y, 1)

            @block.gpsimd
            def _(pool):
                nc.gpsimd.memset(expo[:], -0.5).then_inc(g_pow, 1)
                pool.wait_ge(g_pow, 1)
                with pool.Fori(0, MT) as i:
                    pool.wait_ge(g_tail, i * TAIL + TAIL)
                    nc.gpsimd.tensor_tensor(rstd[:], mv[:, 1:2], expo[:], ALU.pow).then_inc(g_pow, 1)

            @block.scalar
            def _(act):
                with act.Fori(0, MT) as i:
                    with act.Fori(0, H) as h:
                        n = act.snap(i * H + h)
                        act.wait_ge(g_dve, n * STEPS + STEPS)
                        nc.scalar.activation(score[:], score[:], ACT.Exp, bias=neg_max[:],
                                             accum_out=den[:]).then_inc(g_exp, 1)
                        for g in range(TG):
                            act.wait_ge(g_tr, n * TG + (g + 1))
                            nc.scalar.copy(e_t[:, g * 4:(g + 1) * 4, :].rearrange("p a b -> p (a b)"),
                                           ps_e[:, g % 2, :]).then_inc(g_trc, 1)
                    act.wait_ge(g_tail, i * TAIL + 1)
                    nc.scalar.activation(elu_n[:], elu_n[:], ACT.Exp).then_inc(g_elu, 1)

            @block.tensor
            def _(pe):
                with pe.Fori(0, MT) as i:
                    with pe.Fori(0, H) as h:
                        n = pe.snap(i * H + h)
                        pe.wait_ge(g_exp, n + 1)
                        for g in range(TG):
                            if g >= 2:
                                pe.wait_ge(g_trc, n * TG + (g - 1))
                            for t in range(4):
                                m = g * 4 + t
                                last = nc.tensor.transpose(ps_e[:, g % 2, t * P:(t + 1) * P],
                                                           score[:, m * P:(m + 1) * P], ident[:])
                            last.then_inc(g_tr, 1)
                        pe.wait_ge(g_trc, n * TG + TG)
                        pe.wait_ge(g_h, n * 16 + 16)
                        pe.wait_ge(g_free, n + 1)
                        for m in range(MT):
                            last = nc.tensor.matmul(ps_o[:, 0:F], e_t[:, m, :], h_head[:, m, :],
                                                    start=m == 0, stop=m == MT - 1)
                        last.then_inc(g_pv, 1)


def kernel(x, adj, L0_gnn_W, L0_gnn_a1, L0_gnn_a2):
    import numpy as np
    import concourse.bacc as bacc
    from concourse import mybir
    from concourse.bass_utils import run_bass_kernel_spmd

    nc = bacc.Bacc("TRN2", target_bir_lowering=False, num_devices=1)
    x, adj, w = np.asarray(x), np.asarray(adj), np.asarray(L0_gnn_W)
    layouts = {
        "x": x, "x_t": x.T, "adj": adj, "adj_t": adj.T,
        "w": w.transpose(1, 0, 2).reshape(w.shape[1], -1),
        "a1": np.asarray(L0_gnn_a1), "a2": np.asarray(L0_gnn_a2),
    }
    arrays, args = {}, []
    for name, a in layouts.items():
        a = np.ascontiguousarray(a)
        arrays[f"in_{name}"] = a
        args.append(nc.dram_tensor(f"in_{name}", a.shape, mybir.dt.from_np(a.dtype), kind="ExternalInput").ap())
    args.append(nc.dram_tensor("out_y", x.shape, mybir.dt.float32, kind="ExternalOutput").ap())
    build(nc, *args)
    r = run_bass_kernel_spmd(nc, [arrays], core_ids=[0])
    return r.results[0]["out_y"]
```

```python
def build(nc, x, x_t, adj, adj_t, w, a1, a2, out):
    from contextlib import ExitStack

    import concourse.bass as bass
    from concourse import mybir

    f32, f16, i32 = mybir.dt.float32, mybir.dt.float16, mybir.dt.int32
    i8, u8, u32, f8 = mybir.dt.int8, mybir.dt.uint8, mybir.dt.uint32, mybir.dt.float8e4
    ALU = mybir.AluOpType
    ACT = mybir.ActivationFunctionType
    AX = mybir.AxisListType
    RMAX = bass.bass_isa.ReduceOp.max
    ds = bass.ds

    P = 128
    N, D = x.shape
    H = a1.shape[0]
    F = a1.shape[1]
    KT = D // P
    MT = N // P
    CHUNK = 512
    CHUNKS = N // CHUNK
    TPC = CHUNK // P
    SLOPE = 0.2
    F1 = F + 1
    QUADS = 4 * F1
    PAIR = 2 * F1
    BLOCK = 768
    BLOCKS = N // BLOCK
    J = BLOCK // P
    G = 4
    GROUPS = MT // G
    AT = 3
    ALOADS = MT // AT
    DVE_TILES = 1
    RING = 3
    VG = 8
    VLOADS = MT // VG
    LOW = 4096.0
    TOP = 256.0
    ONE = 8
    FLOOR = 2.0 ** -18
    TINY = 1.0e-30
    HUGE = 1.0e30
    NEG_BIG = 9.0e15
    EPS = 1e-5

    h_dram = nc.dram_tensor("h_scratch", [MT, P, D], f32, kind="Internal").ap()
    v_dram = nc.dram_tensor("v_scratch", [H, P, MT, QUADS], f16, kind="Internal").ap()
    s2_dram = nc.dram_tensor("s2_scratch", [H, P, 2 * MT], f32, kind="Internal").ap()
    s_rows_dram = nc.dram_tensor("s_rows_scratch", [2 * H, N], f32, kind="Internal").ap()

    keep = ExitStack()
    with keep:
        def sem(name):
            return keep.enter_context(nc.semaphore(name))

        def kept(name, shape, dt):
            return keep.enter_context(nc.sbuf_tensor(name, shape, dt))

        s_col = kept("s_col", [P, MT, 2 * H], f32)
        ident = kept("ident", [P, P], f32)
        ratio = kept("ratio", [P, H, MT], f32)
        dens = kept("dens", [P, H, MT], f32)
        moments = kept("moments", [P, MT, 2], f32)
        flag = kept("flag", [P, 1], i32)

        with ExitStack() as ph:
            def sb(name, shape, dt):
                return ph.enter_context(nc.sbuf_tensor(name, shape, dt))

            w_sb = sb("w_sb", [P, KT, D], f32)
            a_b = sb("a_b", [P, 2, D], f32)
            wa_prod = sb("wa_prod", [P, 2, D], f32)
            wa = sb("wa", [P, KT, 2 * H], f32)
            xt_sb = sb("xt_sb", [P, KT, N], f32)
            h_sb = sb("h_sb", [P, 2, D], f32)
            s_t = sb("s_t", [2 * H, N], f32)
            s2_pair = sb("s2_pair", [P, H, 2, MT], f32)
            s2_max = sb("s2_max", [P, H], f32)
            c_max = sb("c_max", [P, H], f32)
            bd = sb("bd", [P, 2, MT, H], f32)
            big = sb("big", [P, 3, 2, H, F1], f32)
            vals = sb("vals", [P, 2, H, 4, F1], f16)
            ps_s = ph.enter_context(nc.psum_tensor("ps_s", [P, 1024], f32))
            ps_t = ph.enter_context(nc.psum_tensor("ps_t", [P, 2, CHUNK], f32))
            ps_h = ph.enter_context(nc.psum_tensor("ps_h", [P, 4, D], f32))

            w_loaded, a_loaded, x_loaded = sem("w_loaded"), sem("a_loaded"), [sem(f"x_loaded{c}") for c in range(CHUNKS)]
            id_zero, id_ready = sem("id_zero"), sem("id_ready")
            wa_prod_done, wa_ready = sem("wa_prod_done"), sem("wa_ready")
            s_done, s_col_ready = sem("s_done"), sem("s_col_ready")
            s2_max_ready, c_max_ready, shifted, scaled_up = sem("s2_max_ready"), sem("c_max_ready"), sem("shifted"), sem("scaled_up")
            pairs_ready, exps_done = sem("pairs_ready"), sem("exps_done")
            st_done, st_ready = sem("st_done"), sem("st_ready")
            h_done, h_copied, rows_stored, pairs_stored = sem("h_done"), sem("h_copied"), sem("rows_stored"), sem("pairs_stored")
            big_ready, high_ready, low_ready = sem("big_ready"), sem("high_ready"), sem("low_ready")
            h_stored = [sem("h_stored0"), sem("h_stored1")]
            v_stored = [sem("v_stored0"), sem("v_stored1")]

            block = ph.enter_context(nc.Block())

            @block.sync
            def _(sp):
                sp.dma_start(w_sb[:], w.rearrange("(t p) c -> p t c", p=P)).then_inc(w_loaded, 16)
                for a, src in enumerate((a1, a2)):
                    flat = src.rearrange("h f -> (h f)")[None, :]
                    sp.dma_start(a_b[:, a, :], flat.broadcast_to([P, D])).then_inc(a_loaded, 16)
                for c in range(CHUNKS):
                    part = x_t[:, c * CHUNK:(c + 1) * CHUNK].rearrange("(t p) n -> p t n", p=P)
                    sp.dma_start(xt_sb[:, :, c * CHUNK:(c + 1) * CHUNK], part).then_inc(x_loaded[c], 16)
                sp.wait_ge(pairs_ready, 2)
                sp.dma_start(s2_dram.rearrange("h p c -> p h c"),
                             s2_pair[:].rearrange("p h a m -> p h (a m)")).then_inc(pairs_stored, 16)
                for m in range(MT):
                    sp.wait_ge(h_copied, m + 1)
                    sp.dma_start(h_dram[m], h_sb[:, m % 2, :]).then_inc(h_stored[m % 2], 16)
                    sp.wait_ge(low_ready, 2 * (m + 1))
                    sp.dma_start(v_dram[:, :, m, :].rearrange("h p c -> p h c"),
                                 vals[:, m % 2].rearrange("p h q f -> p h (q f)")).then_inc(v_stored[m % 2], 16)
                sp.wait_ge(st_ready, CHUNKS)
                sp.dma_start(s_rows_dram, s_t[:]).then_inc(rows_stored, 16)
                for slot in range(2):
                    sp.wait_ge(h_stored[slot], 16 * MT // 2)
                    sp.wait_ge(v_stored[slot], 16 * MT // 2)
                sp.wait_ge(rows_stored, 16)
                sp.wait_ge(pairs_stored, 16)

            @block.gpsimd
            def _(pool):
                nc.gpsimd.memset(ident[:], 0.0).then_inc(id_zero, 1)
                pool.wait_ge(id_zero, 1)
                nc.gpsimd.affine_select(out=ident[:], in_=ident[:], compare_op=ALU.not_equal, fill=1.0, base=0,
                                        pattern=[[-1, P]], channel_multiplier=1).then_inc(id_ready, 1)
                pool.wait_ge(s2_max_ready, 1)
                nc.gpsimd.partition_all_reduce(c_max[:], s2_max[:], P, RMAX).then_inc(c_max_ready, 1)

            @block.vector
            def _(dve):
                dve.wait_ge(w_loaded, 16)
                dve.wait_ge(a_loaded, 32)
                for n in range(2 * KT):
                    a, k = n % 2, n // 2
                    if n >= 2:
                        dve.wait_ge(wa_ready, n - 1)
                    nc.vector.tensor_tensor(wa_prod[:, n % 2, :], w_sb[:, k, :], a_b[:, a, :],
                                            ALU.mult).then_inc(wa_prod_done, 1)
                    dve.wait_ge(wa_prod_done, n + 1)
                    nc.vector.tensor_reduce(wa[:, k, a * H:(a + 1) * H],
                                            wa_prod[:, n % 2, :].rearrange("p (h f) -> p h f", f=F),
                                            axis=AX.X, op=ALU.add).then_inc(wa_ready, 1)
                dve.wait_ge(s_done, MT)
                nc.vector.tensor_copy(s_col[:].rearrange("p m s -> p (m s)"),
                                      ps_s[:, 0:MT * 2 * H]).then_inc(s_col_ready, 1)
                dve.wait_ge(s_col_ready, 1)
                s1_hm = s_col[:, :, 0:H].rearrange("p m h -> p h m")
                s2_mh = s_col[:, :, H:2 * H]
                s2_hm = s2_mh.rearrange("p m h -> p h m")
                nc.vector.tensor_reduce(s2_max[:], s2_hm, axis=AX.X, op=ALU.max).then_inc(s2_max_ready, 1)
                nc.vector.tensor_copy(s2_pair[:, :, 0, :], s2_hm).then_inc(pairs_ready, 1)
                nc.vector.tensor_scalar_mul(s2_pair[:, :, 1, :], s2_hm, -1.0).then_inc(pairs_ready, 1)
                dve.wait_ge(c_max_ready, 1)
                c_mh = c_max[:][:, None, :].broadcast_to([P, MT, H])
                c_hm = c_max[:][:, :, None].broadcast_to([P, H, MT])
                nc.vector.tensor_tensor(bd[:, 0], s2_mh, c_mh, ALU.subtract).then_inc(shifted, 1)
                nc.vector.tensor_tensor(ratio[:], s1_hm, c_hm, ALU.add).then_inc(shifted, 1)
                dve.wait_ge(exps_done, 3)
                nc.vector.tensor_scalar_mul(bd[:], bd[:], TOP * LOW).then_inc(scaled_up, 1)
                dve.wait_ge(scaled_up, 1)

                def low_parts(m):
                    dve.wait_ge(high_ready, m + 1)
                    for kind in range(2):
                        nc.vector.scalar_tensor_tensor(out=vals[:, m % 2, :, 2 * kind + 1, :],
                                                       in0=vals[:, m % 2, :, 2 * kind, :], scalar=-LOW,
                                                       in1=big[:, m % 3, kind], op0=ALU.mult,
                                                       op1=ALU.add).then_inc(low_ready, 1)

                for m in range(MT):
                    if m >= 3:
                        dve.wait_ge(low_ready, 2 * (m - 2))
                    dve.wait_ge(h_done, m + 1)
                    for kind in range(2):
                        factor = bd[:, kind, m, :][:, :, None].broadcast_to([P, H, F])
                        nc.vector.tensor_tensor(big[:, m % 3, kind, :, 0:F],
                                                ps_h[:, m % 4, :].rearrange("p (h f) -> p h f", f=F), factor,
                                                ALU.mult).then_inc(big_ready, 1)
                    nc.vector.tensor_copy(big[:, m % 3, :, :, F], bd[:, :, m, :]).then_inc(big_ready, 1)
                    if m >= 1:
                        low_parts(m - 1)
                low_parts(MT - 1)

            @block.tensor
            def _(pe):
                pe.wait_ge(wa_ready, 2 * KT)
                for m in range(MT):
                    if m % TPC == 0:
                        pe.wait_ge(x_loaded[m // TPC], 16)
                    for k in range(KT):
                        last = nc.tensor.matmul(ps_s[:, m * 2 * H:(m + 1) * 2 * H], xt_sb[:, k, m * P:(m + 1) * P],
                                                wa[:, k, :], start=k == 0, stop=k == KT - 1)
                    last.then_inc(s_done, 1)
                for m in range(MT):
                    if m >= 4:
                        pe.wait_ge(h_copied, m - 3)
                        pe.wait_ge(big_ready, 3 * (m - 3))
                    for k in range(KT):
                        last = nc.tensor.matmul(ps_h[:, m % 4, :], xt_sb[:, k, m * P:(m + 1) * P], w_sb[:, k, :],
                                                start=k == 0, stop=k == KT - 1)
                    last.then_inc(h_done, 1)
                    c = m - 4
                    if 0 <= c < CHUNKS:
                        pe.wait_ge(id_ready, 1)
                        pe.wait_ge(s_col_ready, 1)
                        if c >= 2:
                            pe.wait_ge(st_ready, c - 1)
                        for t in range(TPC):
                            last = nc.tensor.transpose(ps_t[0:2 * H, c % 2, t * P:(t + 1) * P],
                                                       s_col[:, c * TPC + t, :], ident[:])
                        last.then_inc(st_done, 1)

            @block.scalar
            def _(act):
                act.wait_ge(shifted, 2)
                nc.scalar.activation(bd[:, 1], bd[:, 0], ACT.Exp, scale=SLOPE).then_inc(exps_done, 1)
                nc.scalar.activation(ratio[:], ratio[:], ACT.Exp, scale=1.0 - SLOPE).then_inc(exps_done, 1)
                act.wait_ge(exps_done, 1)
                nc.scalar.activation(bd[:, 0], bd[:, 0], ACT.Exp).then_inc(exps_done, 1)
                for m in range(MT):
                    c = m - 4
                    if 0 <= c < CHUNKS:
                        act.wait_ge(st_done, c + 1)
                        nc.scalar.copy(s_t[:, c * CHUNK:(c + 1) * CHUNK],
                                       ps_t[0:2 * H, c % 2, :]).then_inc(st_ready, 1)
                    act.wait_ge(big_ready, 3 * (m + 1))
                    if m >= 2:
                        act.wait_ge(v_stored[m % 2], 16 * (m // 2))
                    for kind in range(2):
                        last = nc.scalar.mul(vals[:, m % 2, :, 2 * kind, :], big[:, m % 3, kind], 1.0 / LOW)
                    last.then_inc(high_ready, 1)
                    if m >= 2:
                        act.wait_ge(h_stored[m % 2], 16 * (m // 2))
                    nc.scalar.copy(h_sb[:, m % 2, :], ps_h[:, m % 4, :]).then_inc(h_copied, 1)

        with ExitStack() as ph:
            def sb(name, shape, dt):
                return ph.enter_context(nc.sbuf_tensor("m_" + name, shape, dt))

            adj_one = sb("adj_one", [P, 2, MT, BLOCK], u8)
            stage = sb("stage", [P, 2, AT, BLOCK], i32)
            vals = sb("vals", [P, MT, QUADS], f16)
            s1_b = sb("s1_b", [P, 2, BLOCK], f32)
            s2_c = sb("s2_c", [P, 2, 2, MT], f32)
            sign = sb("sign", [P, RING, G, BLOCK], i8)
            neg = sb("neg", [P, RING, G, BLOCK], u8)
            pos = sb("pos", [P, RING, G, BLOCK], u8)
            pos_sum = sb("pos_sum", [P, J, PAIR], f32)
            both = sb("both", [P, J, PAIR], f32)
            total = sb("total", [P, J, F1], f32)
            den = sb("den", [P, J], f32)
            rden = sb("rden", [P, J], f32)
            att = sb("att", [P, J, D], f32)
            xz = sb("xz", [P, J, D], f32)
            ey = sb("ey", [P, J, D], f32)
            stats = sb("stats", [P, J, 6], f32)
            mv = sb("mv", [P, J, 2], f32)
            spread = sb("spread", [P, J], f32)
            rstd = sb("rstd", [P, J], f32)
            expo = sb("expo", [P, J], f32)
            ok = sb("ok", [P, H, MT], f32)
            ok_v = sb("ok_v", [P, MT], f32)
            fails = sb("fails", [P, 2], f32)
            fail = sb("fail", [P, 1], f32)
            fail_all = sb("fail_all", [P, 1], f32)
            acc = ph.enter_context(nc.psum_tensor("acc", [P, 2, 4, 512], f32))

            row_loaded = [sem("row_loaded0"), sem("row_loaded1")]
            v_loaded = [sem(f"v_loaded{k}") for k in range(VLOADS)]
            adj_loaded = [sem("adj_loaded0"), sem("adj_loaded1")]
            adj_ready = sem("adj_ready")
            sign_act = sem("sign_act")
            sign_dve = sem("sign_dve")
            neg_ready = sem("neg_ready")
            masks_ready = sem("masks_ready")
            masks_used = sem("masks_used")
            pos_scaled = sem("pos_scaled")
            acc_free = sem("acc_free")
            both_ready, total_ready, den_ready, rden_ready = sem("both_ready"), sem("total_ready"), sem("den_ready"), sem("rden_ready")
            att_ready = sem("att_ready")
            x_in, pos_added, min_ready, exp_ready = sem("x_in"), sem("pos_added"), sem("min_ready"), sem("exp_ready")
            z_ready, stats_ready, var_ready, eps_added, pow_ready = sem("z_ready"), sem("stats_ready"), sem("var_ready"), sem("eps_added"), sem("pow_ready")
            y_ready, y_stored, consts = sem("y_ready"), sem("y_stored"), sem("consts")
            checked, fail_ready, fail_max = sem("checked"), sem("fail_ready"), sem("fail_max")
            flag_ready = sem("flag_ready")

            block = ph.enter_context(nc.Block())
            HEADS = BLOCKS * H

            def row_tiles(dram, b):
                return dram[ds(b * BLOCK, BLOCK), :].rearrange("(j p) c -> p j c", p=P)

            @block.sync
            def _(sp):
                def load_row(b, h, par):
                    sp.dma_start(s1_b[:, par, :], s_rows_dram[ds(h, 1), ds(b * BLOCK, BLOCK)]
                                 .broadcast_to([P, BLOCK])).then_inc(row_loaded[par], 16)
                    sp.dma_start(s2_c[:, par].rearrange("p a m -> p (a m)"),
                                 s2_dram[ds(h, 1)].rearrange("a p c -> (a p) c")).then_inc(row_loaded[par], 16)

                def load_values(h, k):
                    sp.dma_start(vals[:, k * VG:(k + 1) * VG, :],
                                 v_dram[ds(h, 1), :, k * VG:(k + 1) * VG, :]
                                 .rearrange("a p m c -> (a p) m c")).then_inc(v_loaded[k], 16)

                def load_adj(b, c, slot):
                    sp.dma_start(stage[:, slot], adj_t[ds(c * (AT * P), AT * P), ds(b * BLOCK, BLOCK)]
                                 .rearrange("(t p) n -> p t n", p=P)).then_inc(adj_loaded[slot], 16)

                for c in range(ALOADS):
                    if c >= 2:
                        sp.wait_ge(adj_ready, c - 1)
                    load_adj(0, c, c % 2)
                    if c == 0:
                        load_row(0, 0, 0)
                    if c < VLOADS:
                        load_values(0, c)
                sp.dma_start(xz[:], row_tiles(x, 0)).then_inc(x_in, 16)
                sp.sem_inc(y_stored, 16)
                with sp.Fori(0, BLOCKS) as b:
                    with sp.Fori(0, H // 2) as hp:
                        for par in range(2):
                            n = sp.snap(b * H + hp * 2 + par)
                            for k in range(VLOADS):
                                sp.wait_ge(masks_used, n * GROUPS + (2 * (k + 1) + RING))
                                load_values((hp * 2 + (par + 1)) % H, k)
                                if k == 1 and par == 0:
                                    load_row(b, hp * 2 + 1, 1)
                                if k == 1 and par == 1:
                                    with sp.If(n < HEADS - 1):
                                        load_row(((n + 1) // H) % BLOCKS, (hp * 2 + 2) % H, 0)
                                if k % 3 == 2:
                                    i = 2 * par + k // 3
                                    with sp.If(b < BLOCKS - 1):
                                        sp.wait_ge(adj_ready, (b + 1) * ALOADS + hp * 4 + (i - 1))
                                        load_adj((b + 1) % BLOCKS, hp * 4 + i, i % 2)
                                if k == 4 and par == 0:
                                    with sp.If((hp == 1) * (b > 0) != 0):
                                        sp.wait_ge(y_ready, b * J)
                                        sp.dma_start(row_tiles(out, (b + (BLOCKS - 1)) % BLOCKS), ey[:]).then_inc(y_stored, 16)
                                        sp.dma_start(xz[:], row_tiles(x, b)).then_inc(x_in, 16)
                for k in range(VLOADS):
                    sp.wait_ge(v_loaded[k], 16 * (HEADS + 1))
                sp.wait_ge(y_ready, BLOCKS * J)
                sp.dma_start(row_tiles(out, BLOCKS - 1), ey[:]).then_inc(y_stored, 16)
                sp.wait_ge(y_stored, 16 * (BLOCKS + 1))

            @block.gpsimd
            def _(pool):
                loads = [pool.alloc_register(f"adj_loads{slot}") for slot in range(2)]
                heads = pool.alloc_register("heads_done")
                for slot in range(2):
                    pool.reg_mov(loads[slot], 8 * ALOADS + 16)
                pool.reg_mov(heads, H)

                def convert(par, c, b=None):
                    arrived = pool.snap(loads[c % 2])
                    if b is not None:
                        pool.wait_ge(masks_ready, b * (H * GROUPS))
                    pool.wait_ge(adj_loaded[c % 2], arrived)
                    pool.reg_add(loads[c % 2], loads[c % 2], 16)
                    nc.gpsimd.tensor_scalar(adj_one[:, par, c * AT:(c + 1) * AT, :], stage[:, c % 2], 0.0, float(ONE),
                                            ALU.is_gt, ALU.mult).then_inc(adj_ready, 1)

                def take_min(b):
                    complete = pool.snap(heads)
                    pool.wait_ge(y_stored, b * 16 + 16)
                    pool.wait_ge(att_ready, complete)
                    pool.reg_add(heads, heads, H)
                    nc.gpsimd.tensor_scalar_min(ey[:], att[:], 0.0).then_inc(min_ready, 1)

                def take_pow(b):
                    pool.wait_ge(eps_added, b + 1)
                    nc.gpsimd.tensor_tensor(rstd[:], spread[:], expo[:], ALU.pow).then_inc(pow_ready, 1)

                nc.gpsimd.memset(expo[:], -0.5).then_inc(consts, 1)
                pool.wait_ge(consts, 1)
                pool.sem_inc(min_ready, 1)
                for c in range(ALOADS):
                    convert(1, c)
                with pool.Fori(0, (BLOCKS - 2) // 2) as i:
                    for par in range(2):
                        b = pool.snap(i * 2 + (1 + par))
                        take_min(b - 1)
                        for c in range(ALOADS):
                            convert(par, c, b if c == 0 else None)
                            if c == 2:
                                take_pow(b - 1)
                for b in (BLOCKS - 2, BLOCKS - 1):
                    take_min(b)
                    take_pow(b)
                pool.wait_ge(fail_ready, 1)
                nc.gpsimd.partition_all_reduce(fail_all[:], fail[:], P, RMAX).then_inc(fail_max, 1)

            @block.scalar
            def _(act):
                def scale_pos(m, par):
                    act.wait_ge(masks_used, m * GROUPS + (GROUPS + RING))
                    act.wait_ge(acc_free, m + 2)
                    for j in range(J):
                        row = ratio[:, ds(m % H, 1), ds((m // H) * J + j, 1)].rearrange("p a b -> p (a b)")
                        last = nc.scalar.activation(pos_sum[:, j, :],
                                                    acc[:, par, j // 3, (j % 3) * PAIR:(j % 3 + 1) * PAIR],
                                                    ACT.Identity, scale=row)
                    last.then_inc(pos_scaled, 1)

                def take_exp(b):
                    act.wait_ge(min_ready, b + 2)
                    nc.scalar.activation(ey[:], ey[:], ACT.Exp).then_inc(exp_ready, 1)

                with act.Fori(0, BLOCKS) as b:
                    with act.Fori(0, H // 2) as hp:
                        for par in range(2):
                            n = act.snap(b * H + hp * 2 + par)
                            first = act.snap(n * GROUPS)
                            act.wait_ge(row_loaded[par], (b * (H // 2) + hp) * 32 + 32)
                            for g in range(GROUPS):
                                act.wait_ge(neg_ready, first + (g + 1))
                                for t in range(DVE_TILES, G):
                                    m = g * G + t
                                    last = nc.scalar.activation(sign[:, g % RING, t, :], s1_b[:, par, :], ACT.Sign,
                                                                bias=s2_c[:, par, 0, m:m + 1])
                                last.then_inc(sign_act, 1)
                                if g == 3 and par == 1:
                                    scale_pos(n - 1, 0)
                                if g == 3 and par == 0:
                                    with act.If(n > 0):
                                        scale_pos((n + (HEADS - 1)) % HEADS, 1)
                                if g == 10 and par == 0:
                                    with act.If((hp == 0) * (b > 0) != 0):
                                        take_exp((b + (BLOCKS - 1)) % BLOCKS)
                scale_pos(HEADS - 1, 1)
                take_exp(BLOCKS - 1)

            @block.vector
            def _(dve):
                def signs(par, g):
                    for t in range(DVE_TILES):
                        m = g * G + t
                        last = nc.vector.tensor_scalar(sign[:, g % RING, t, :].bitcast(u8), s1_b[:, par, :],
                                                       s2_c[:, par, 1, m:m + 1], 128.0, ALU.is_lt, ALU.mult)
                    last.then_inc(sign_dve, 1)

                def gather(m, par):
                    dve.wait_ge(pos_scaled, m + 1)
                    for half in range(2):
                        nc.vector.tensor_tensor(both[:, 3 * half:3 * half + 3, :].rearrange("p j c -> p (j c)"),
                                                acc[:, par, 2 + half, 0:3 * PAIR],
                                                pos_sum[:, 3 * half:3 * half + 3, :].rearrange("p j c -> p (j c)"),
                                                ALU.add).then_inc(both_ready if half == 0 else acc_free, 1)
                    dve.wait_ge(both_ready, m + 1)
                    dve.wait_ge(acc_free, m + 3)
                    nc.vector.scalar_tensor_tensor(out=total[:], in0=both[:, :, F1:PAIR], scalar=1.0 / LOW,
                                                   in1=both[:, :, 0:F1], op0=ALU.mult,
                                                   op1=ALU.add).then_inc(total_ready, 1)
                    dve.wait_ge(total_ready, m + 1)
                    nc.vector.tensor_scalar_max(den[:], total[:, :, F], TINY).then_inc(den_ready, 1)
                    dve.wait_ge(den_ready, m + 1)
                    nc.vector.reciprocal(rden[:], den[:]).then_inc(rden_ready, 1)
                    nc.vector.tensor_copy(dens[:, ds(m % H, 1), ds((m // H) * J, J)], den[:][:, None, :])
                    dve.wait_ge(min_ready, m // H + 1)
                    dve.wait_ge(rden_ready, m + 1)
                    nc.vector.tensor_tensor(att[:, :, ds((m % H) * F, F)], total[:, :, 0:F],
                                            rden[:][:, :, None].broadcast_to([P, J, F]),
                                            ALU.mult).then_inc(att_ready, 1)

                def add_positive(b):
                    dve.wait_ge(att_ready, b * H + H)
                    dve.wait_ge(x_in, b * 16 + 16)
                    nc.vector.scalar_tensor_tensor(out=xz[:], in0=att[:], scalar=0.0, in1=xz[:], op0=ALU.max,
                                                   op1=ALU.add).then_inc(pos_added, 1)

                def add_negative(b):
                    dve.wait_ge(pos_added, b + 1)
                    dve.wait_ge(exp_ready, b + 1)
                    nc.vector.scalar_tensor_tensor(out=xz[:], in0=ey[:], scalar=-1.0, in1=xz[:], op0=ALU.add,
                                                   op1=ALU.add).then_inc(z_ready, 1)

                def row_stats(b):
                    dve.wait_ge(z_ready, b + 1)
                    for j in range(J):
                        nc.vector.bn_stats(stats[:, j, :], xz[:, j, :])
                    dve.drain()
                    for j in range(J):
                        last = nc.vector.bn_aggr(mv[:, j, :], stats[:, j, :])
                    last.then_inc(var_ready, 1)
                    dve.wait_ge(var_ready, b + 1)
                    nc.vector.tensor_scalar_add(spread[:], mv[:, :, 1], EPS).then_inc(eps_added, 1)
                    nc.vector.tensor_copy(moments[:, ds(b * J, J), :], mv[:])

                def normalise(b):
                    dve.wait_ge(pow_ready, b + 1)
                    for j in range(J):
                        nc.vector.tensor_scalar(ey[:, j, :], xz[:, j, :], mv[:, j, 0:1], rstd[:, j:j + 1],
                                                ALU.subtract, ALU.mult).then_inc(y_ready, 1)

                dve.sem_inc(neg_ready, RING)
                dve.sem_inc(acc_free, 2)
                for c in range(ALOADS):
                    dve.wait_ge(adj_loaded[c % 2], 16 * (c // 2 + 1))
                    nc.vector.tensor_scalar(adj_one[:, 0, c * AT:(c + 1) * AT, :], stage[:, c % 2], 0.0, float(ONE),
                                            ALU.is_gt, ALU.mult).then_inc(adj_ready, 1)
                with dve.Fori(0, BLOCKS) as b:
                    b_par = dve.snap(b % 2)
                    with dve.Fori(0, H // 2) as hp:
                        for par in range(2):
                            n = dve.snap(b * H + hp * 2 + par)
                            first = dve.snap(n * GROUPS)
                            if par == 0:
                                dve.wait_ge(adj_ready, b * ALOADS + ALOADS)
                            dve.wait_ge(row_loaded[par], (b * (H // 2) + hp) * 32 + 32)
                            signs(par, 0)
                            for g in range(GROUPS):
                                words = [t[:, g % RING].rearrange("p t n -> p (t n)").bitcast(u32)
                                         for t in (sign, neg, pos)]
                                near = adj_one[:, ds(b_par, 1), g * G:(g + 1) * G, :] \
                                    .rearrange("p a t n -> p (a t n)").bitcast(u32)
                                dve.wait_ge(masks_used, first + (g + 1))
                                dve.wait_ge(sign_dve, first + (g + 1))
                                dve.wait_ge(sign_act, first + (g + 1))
                                nc.vector.scalar_tensor_tensor(out=words[1], in0=words[0], scalar=4, in1=near,
                                                               op0=ALU.logical_shift_right,
                                                               op1=ALU.bitwise_and).then_inc(neg_ready, 1)
                                if g < GROUPS - 1:
                                    signs(par, g + 1)
                                dve.wait_ge(neg_ready, first + (g + 1 + RING))
                                nc.vector.tensor_tensor(words[2], words[1], near, ALU.bitwise_xor) \
                                    .then_inc(masks_ready, 1)
                                if g == 4 and par == 1:
                                    gather(n - 1, 0)
                                if g == 4 and par == 0:
                                    with dve.If(n > 0):
                                        gather((n + (HEADS - 1)) % HEADS, 1)
                                if g == 5 and par == 0:
                                    with dve.If((hp == 0) * (b > 0) != 0):
                                        add_positive((b + (BLOCKS - 1)) % BLOCKS)
                                if g == 1 and par == 1:
                                    with dve.If((hp == 0) * (b > 0) != 0):
                                        add_negative((b + (BLOCKS - 1)) % BLOCKS)
                                if g == 3 and par == 1:
                                    with dve.If((hp == 0) * (b > 0) != 0):
                                        row_stats((b + (BLOCKS - 1)) % BLOCKS)
                                if g == 1 and par == 0:
                                    with dve.If((hp == 1) * (b > 0) != 0):
                                        normalise((b + (BLOCKS - 1)) % BLOCKS)
                last_block = BLOCKS - 1
                gather(HEADS - 1, 1)
                add_positive(last_block)
                add_negative(last_block)
                row_stats(last_block)
                normalise(last_block)

                nc.vector.tensor_scalar(ok[:], ratio[:], 1.0, FLOOR, ALU.add, ALU.mult).then_inc(checked, 1)
                dve.wait_ge(checked, 1)
                nc.vector.tensor_tensor(ok[:], dens[:], ok[:], ALU.is_ge).then_inc(checked, 1)
                dve.wait_ge(checked, 2)
                nc.vector.scalar_tensor_tensor(out=ok[:], in0=dens[:], scalar=HUGE, in1=ok[:], op0=ALU.is_le,
                                               op1=ALU.mult).then_inc(checked, 1)
                nc.vector.tensor_scalar(ok_v[:], moments[:, :, 1], HUGE, None, ALU.is_le).then_inc(checked, 1)
                dve.wait_ge(checked, 4)
                nc.vector.tensor_reduce(fails[:, 0:1], ok[:].rearrange("p h m -> p (h m)"), axis=AX.X,
                                        op=ALU.min).then_inc(checked, 1)
                nc.vector.tensor_reduce(fails[:, 1:2], ok_v[:], axis=AX.X, op=ALU.min).then_inc(checked, 1)
                dve.wait_ge(checked, 6)
                nc.vector.tensor_tensor(fail[:], fails[:, 0:1], fails[:, 1:2], ALU.min).then_inc(checked, 1)
                dve.wait_ge(checked, 7)
                nc.vector.tensor_scalar(fail[:], fail[:], -1.0, 1.0, ALU.mult, ALU.add).then_inc(fail_ready, 1)
                dve.wait_ge(fail_max, 1)
                nc.vector.tensor_copy(flag[:], fail_all[:]).then_inc(flag_ready, 1)

            @block.tensor
            def _(pe):
                pe.sem_inc(masks_used, RING)
                count = pe.alloc_register("group_count")
                pe.reg_mov(count, 1)
                with pe.Fori(0, HEADS // 2) as i:
                    for par in range(2):
                        for g in range(GROUPS):
                            upto = pe.snap(count)
                            if g == 0:
                                pe.wait_ge(acc_free, i * 2 + (par + 1))
                            if g % 2 == 0:
                                pe.wait_ge(v_loaded[g // 2], i * 32 + 16 * (par + 1))
                            pe.wait_ge(masks_ready, upto)
                            pe.reg_add(count, count, 1)
                            for t in range(G):
                                m = g * G + t
                                for j in range(J):
                                    for side, mask in enumerate((pos, neg)):
                                        last = nc.tensor.matmul(
                                            acc[:, par, 2 * side + j // 3, (j % 3) * PAIR:(j % 3 + 1) * PAIR],
                                            mask[:, g % RING, t, j * P:(j + 1) * P].bitcast(f8),
                                            vals[:, m, side * PAIR:(side + 1) * PAIR],
                                            start=m == 0 and j % 3 == 0, stop=m == MT - 1,
                                            skip_group_check=True)
                            last.then_inc(masks_used, 1)

        with ExitStack() as ph:
            def sb(name, shape, dt):
                return ph.enter_context(nc.sbuf_tensor("g_" + name, shape, dt))

            adj_row = sb("adj_row", [P, N], i32)
            mask = sb("mask", [P, N], f32)
            s2_b = sb("s2_b", [P, N], f32)
            score = sb("score", [P, N], f32)
            e_t = sb("e_t", [P, MT, P], f32)
            h_head = sb("h_head", [P, MT, F], f32)
            x_row = sb("x_row", [P, D], f32)
            att = sb("att", [P, D], f32)
            elu_n = sb("elu_n", [P, D], f32)
            y_row = sb("y_row", [P, D], f32)
            neg_max = sb("neg_max", [P, 1], f32)
            den = sb("den", [P, 1], f32)
            rden = sb("rden", [P, 1], f32)
            stats = sb("stats", [P, 6], f32)
            mv = sb("mv", [P, 2], f32)
            rstd = sb("rstd", [P, 1], f32)
            expo = sb("expo", [P, 1], f32)
            neg_off = adj_row[:].bitcast(f32)
            scaled = e_t[:].rearrange("p m n -> p (m n)")
            ps_e = ph.enter_context(nc.psum_tensor("ps_e", [P, 2, 4 * P], f32))
            ps_o = ph.enter_context(nc.psum_tensor("ps_o", [P, 512], f32))
            TG = MT // 4

            g_adj, g_x, g_s2, g_h = sem("g_adj"), sem("g_x"), sem("g_s2"), sem("g_h")
            g_mask, g_off = sem("g_mask"), sem("g_off")
            g_dve, g_exp, g_tr, g_trc, g_pv = sem("g_dve"), sem("g_exp"), sem("g_tr"), sem("g_trc"), sem("g_pv")
            g_tail, g_elu, g_pow, g_y, g_out = sem("g_tail"), sem("g_elu"), sem("g_pow"), sem("g_y"), sem("g_out")
            g_ex, g_free = sem("g_ex"), sem("g_free")
            block = ph.enter_context(nc.Block())
            STEPS = 5
            TAIL = 6

            @block.sync
            def _(sp):
                redo = sp.value_load(flag[0:1, 0:1])
                with sp.If(redo != 0):
                    sp.sem_inc(g_free, 1)
                    sp.sem_inc(g_out, 16)
                    with sp.Fori(0, MT) as i:
                        sp.dma_start(adj_row[:], adj[ds(i * P, P), :]).then_inc(g_adj, 16)
                        sp.dma_start(x_row[:], x[ds(i * P, P), :]).then_inc(g_x, 16)
                        with sp.Fori(0, H) as h:
                            sp.wait_ge(g_free, i * H + h + 1)
                            sp.dma_start(s2_b[:], s_rows_dram[ds(h + H, 1), :].broadcast_to([P, N])).then_inc(g_s2, 16)
                            sp.dma_start(h_head[:], h_dram.rearrange("m p (h f) -> h p m f", f=F)[ds(h, 1)]
                                         .rearrange("a p m f -> (a p) m f")).then_inc(g_h, 16)
                        sp.wait_ge(g_y, i + 1)
                        sp.dma_start(out[ds(i * P, P), :], y_row[:]).then_inc(g_out, 16)
                    sp.wait_ge(g_out, 16 * MT + 16)

            @block.vector
            def _(dve):
                redo = dve.value_load(flag[0:1, 0:1])
                with dve.If(redo != 0):
                    with dve.Fori(0, MT) as i:
                        dve.wait_ge(g_adj, i * 16 + 16)
                        nc.vector.tensor_scalar(mask[:], adj_row[:], 0.0, None, ALU.is_gt).then_inc(g_mask, 1)
                        dve.wait_ge(g_mask, i + 1)
                        nc.vector.tensor_scalar(neg_off, mask[:], -1.0, NEG_BIG, ALU.add, ALU.mult).then_inc(g_off, 1)
                        with dve.Fori(0, H) as h:
                            n = dve.snap(i * H + h)
                            base = dve.snap(n * STEPS)
                            s1 = s_col[:, ds(i, 1), ds(h, 1)].rearrange("p a b -> p (a b)")
                            dve.wait_ge(g_s2, n * 16 + 16)
                            nc.vector.tensor_scalar(scaled, s2_b[:], s1, SLOPE, ALU.add, ALU.mult).then_inc(g_dve, 1)
                            dve.wait_ge(g_dve, base + 1)
                            nc.vector.scalar_tensor_tensor(out=score[:], in0=s2_b[:], scalar=s1, in1=scaled,
                                                           op0=ALU.add, op1=ALU.max).then_inc(g_dve, 1)
                            dve.wait_ge(g_dve, base + 2)
                            nc.vector.tensor_tensor(score[:], score[:], mask[:], ALU.mult).then_inc(g_dve, 1)
                            dve.wait_ge(g_off, i + 1)
                            dve.wait_ge(g_dve, base + 3)
                            nc.vector.tensor_tensor(score[:], score[:], neg_off, ALU.add).then_inc(g_dve, 1)
                            dve.wait_ge(g_dve, base + 4)
                            nc.vector.tensor_reduce(neg_max[:], score[:], axis=AX.X, op=ALU.max, negate=True).then_inc(g_dve, 1)
                            dve.wait_ge(g_exp, n + 1)
                            nc.vector.reciprocal(rden[:], den[:]).then_inc(g_ex, 1)
                            dve.wait_ge(g_ex, n + 1)
                            dve.wait_ge(g_pv, n + 1)
                            nc.vector.tensor_scalar(att[:, ds(h * F, F)], ps_o[:, 0:F], rden[:], None,
                                                    ALU.mult).then_inc(g_free, 1)
                        tail = dve.snap(i * TAIL)
                        dve.wait_ge(g_free, i * H + H + 1)
                        nc.vector.tensor_scalar_min(elu_n[:], att[:], 0.0).then_inc(g_tail, 1)
                        dve.wait_ge(g_elu, i + 1)
                        dve.wait_ge(g_x, i * 16 + 16)
                        nc.vector.scalar_tensor_tensor(out=elu_n[:], in0=elu_n[:], scalar=-1.0, in1=x_row[:],
                                                       op0=ALU.add, op1=ALU.add).then_inc(g_tail, 1)
                        dve.wait_ge(g_tail, tail + 2)
                        nc.vector.scalar_tensor_tensor(out=att[:], in0=att[:], scalar=0.0, in1=elu_n[:],
                                                       op0=ALU.max, op1=ALU.add).then_inc(g_tail, 1)
                        dve.wait_ge(g_tail, tail + 3)
                        nc.vector.bn_stats(stats[:], att[:]).then_inc(g_tail, 1)
                        dve.drain()
                        nc.vector.bn_aggr(mv[:], stats[:]).then_inc(g_tail, 1)
                        dve.wait_ge(g_tail, tail + 5)
                        nc.vector.tensor_scalar_add(mv[:, 1:2], mv[:, 1:2], EPS).then_inc(g_tail, 1)
                        dve.wait_ge(g_out, i * 16 + 16)
                        dve.wait_ge(g_pow, i + 2)
                        nc.vector.tensor_scalar(y_row[:], att[:], mv[:, 0:1], rstd[:], ALU.subtract,
                                                ALU.mult).then_inc(g_y, 1)

            @block.gpsimd
            def _(pool):
                redo = pool.value_load(flag[0:1, 0:1])
                with pool.If(redo != 0):
                    nc.gpsimd.memset(expo[:], -0.5).then_inc(g_pow, 1)
                    pool.wait_ge(g_pow, 1)
                    with pool.Fori(0, MT) as i:
                        pool.wait_ge(g_tail, i * TAIL + TAIL)
                        nc.gpsimd.tensor_tensor(rstd[:], mv[:, 1:2], expo[:], ALU.pow).then_inc(g_pow, 1)

            @block.scalar
            def _(act):
                redo = act.value_load(flag[0:1, 0:1])
                with act.If(redo != 0):
                    with act.Fori(0, MT) as i:
                        with act.Fori(0, H) as h:
                            n = act.snap(i * H + h)
                            act.wait_ge(g_dve, n * STEPS + STEPS)
                            nc.scalar.activation(score[:], score[:], ACT.Exp, bias=neg_max[:],
                                                 accum_out=den[:]).then_inc(g_exp, 1)
                            for g in range(TG):
                                act.wait_ge(g_tr, n * TG + (g + 1))
                                nc.scalar.copy(e_t[:, g * 4:(g + 1) * 4, :].rearrange("p a b -> p (a b)"),
                                               ps_e[:, g % 2, :]).then_inc(g_trc, 1)
                        act.wait_ge(g_tail, i * TAIL + 1)
                        nc.scalar.activation(elu_n[:], elu_n[:], ACT.Exp).then_inc(g_elu, 1)

            @block.tensor
            def _(pe):
                redo = pe.value_load(flag[0:1, 0:1])
                with pe.If(redo != 0):
                    with pe.Fori(0, MT) as i:
                        with pe.Fori(0, H) as h:
                            n = pe.snap(i * H + h)
                            pe.wait_ge(g_exp, n + 1)
                            for g in range(TG):
                                if g >= 2:
                                    pe.wait_ge(g_trc, n * TG + (g - 1))
                                for t in range(4):
                                    m = g * 4 + t
                                    last = nc.tensor.transpose(ps_e[:, g % 2, t * P:(t + 1) * P],
                                                               score[:, m * P:(m + 1) * P], ident[:])
                                last.then_inc(g_tr, 1)
                            pe.wait_ge(g_trc, n * TG + TG)
                            pe.wait_ge(g_h, n * 16 + 16)
                            pe.wait_ge(g_free, n + 1)
                            for m in range(MT):
                                last = nc.tensor.matmul(ps_o[:, 0:F], e_t[:, m, :], h_head[:, m, :],
                                                        start=m == 0, stop=m == MT - 1)
                            last.then_inc(g_pv, 1)


def kernel(x, adj, L0_gnn_W, L0_gnn_a1, L0_gnn_a2):
    import numpy as np
    import concourse.bacc as bacc
    from concourse import mybir
    from concourse.bass_utils import run_bass_kernel_spmd

    nc = bacc.Bacc("TRN2", target_bir_lowering=False, num_devices=1)
    x, adj, w = np.asarray(x), np.asarray(adj), np.asarray(L0_gnn_W)
    layouts = {
        "x": x, "x_t": x.T, "adj": adj, "adj_t": adj.T,
        "w": w.transpose(1, 0, 2).reshape(w.shape[1], -1),
        "a1": np.asarray(L0_gnn_a1), "a2": np.asarray(L0_gnn_a2),
    }
    arrays, args = {}, []
    for name, a in layouts.items():
        a = np.ascontiguousarray(a)
        arrays[f"in_{name}"] = a
        args.append(nc.dram_tensor(f"in_{name}", a.shape, mybir.dt.from_np(a.dtype), kind="ExternalInput").ap())
    args.append(nc.dram_tensor("out_y", x.shape, mybir.dt.float32, kind="ExternalOutput").ap())
    build(nc, *args)
    r = run_bass_kernel_spmd(nc, [arrays], core_ids=[0])
    return r.results[0]["out_y"]
```

```python
def build(nc, x, x_t, adj, adj_t, w, a1, a2, out):
    from contextlib import ExitStack

    import concourse.bass as bass
    from concourse import mybir

    f32, f16, i32 = mybir.dt.float32, mybir.dt.float16, mybir.dt.int32
    i8, u8, u32, f8 = mybir.dt.int8, mybir.dt.uint8, mybir.dt.uint32, mybir.dt.float8e4
    ALU = mybir.AluOpType
    ACT = mybir.ActivationFunctionType
    AX = mybir.AxisListType
    RMAX = bass.bass_isa.ReduceOp.max
    ds = bass.ds

    P = 128
    N, D = x.shape
    H = a1.shape[0]
    F = a1.shape[1]
    KT = D // P
    MT = N // P
    CHUNK = 512
    CHUNKS = N // CHUNK
    TPC = CHUNK // P
    SLOPE = 0.2
    F1 = F + 1
    QUADS = 4 * F1
    PAIR = 2 * F1
    BLOCK = 768
    BLOCKS = N // BLOCK
    J = BLOCK // P
    G = 4
    GROUPS = MT // G
    AT = 2
    ALOADS = MT // AT
    DVE_TILES = (1, 2, 1, 1, 1, 1, 1, 1, 1, 1, 1, 1)
    AT_SCALE, AT_GATHER = 6, 6
    AT_ADD = 9
    RING = 4
    SIGNS = 3
    VG = 12
    VLOADS = MT // VG
    LOW = 4096.0
    TOP = 256.0
    ONE = 8
    FLOOR = 2.0 ** -18
    TINY = 1.0e-30
    HUGE = 1.0e30
    NEG_BIG = 9.0e15
    EPS = 1e-5

    h_dram = nc.dram_tensor("h_scratch", [MT, P, D], f32, kind="Internal").ap()
    v_dram = nc.dram_tensor("v_scratch", [H, P, MT, QUADS], f16, kind="Internal").ap()
    s2_dram = nc.dram_tensor("s2_scratch", [H, P, 2 * MT], f32, kind="Internal").ap()
    s_rows_dram = nc.dram_tensor("s_rows_scratch", [2 * H, N], f32, kind="Internal").ap()

    keep = ExitStack()
    with keep:
        def sem(name):
            return keep.enter_context(nc.semaphore(name))

        def kept(name, shape, dt):
            return keep.enter_context(nc.sbuf_tensor(name, shape, dt))

        s_col = kept("s_col", [P, MT, 2 * H], f32)
        ident = kept("ident", [P, P], f32)
        ratio = kept("ratio", [P, H, MT], f32)
        dens = kept("dens", [P, H, MT], f32)
        moments = kept("moments", [P, MT, 2], f32)
        flag = kept("flag", [P, 1], i32)
        edges = ExitStack()
        adj_one = edges.enter_context(nc.sbuf_tensor("adj_one", [P, 2, MT, BLOCK], u8))
        stage = edges.enter_context(nc.sbuf_tensor("stage", [P, 2, AT, BLOCK], i32))
        s1_b = edges.enter_context(nc.sbuf_tensor("s1_b", [P, 2, BLOCK], f32))
        s2_c = edges.enter_context(nc.sbuf_tensor("s2_c", [P, 2, 2, MT], f32))
        row_loaded = [sem("row_loaded0"), sem("row_loaded1")]
        adj_loaded = [sem("adj_loaded0"), sem("adj_loaded1")]
        adj_ready = sem("adj_ready")

        def load_adj(sp, b, c, slot):
            sp.dma_start(stage[:, slot], adj_t[ds(c * (AT * P), AT * P), ds(b * BLOCK, BLOCK)]
                         .rearrange("(t p) n -> p t n", p=P)).then_inc(adj_loaded[slot], 16)

        def load_row(sp, b, h, par):
            sp.dma_start(s1_b[:, par, :], s_rows_dram[ds(h, 1), ds(b * BLOCK, BLOCK)]
                         .broadcast_to([P, BLOCK])).then_inc(row_loaded[par], 16)
            sp.dma_start(s2_c[:, par].rearrange("p a m -> p (a m)"),
                         s2_dram[ds(h, 1)].rearrange("a p c -> (a p) c")).then_inc(row_loaded[par], 16)

        def to_bytes(par, c):
            nc.gpsimd.tensor_scalar(adj_one[:, par, c * AT:(c + 1) * AT, :], stage[:, c % 2], 0.0, float(ONE),
                                    ALU.is_gt, ALU.mult).then_inc(adj_ready, 1)

        with ExitStack() as ph:
            def sb(name, shape, dt):
                return ph.enter_context(nc.sbuf_tensor(name, shape, dt))

            room, taken = adj_one[:, 1].rearrange("p m n -> p (m n)"), [0]

            def share(count, dt, size):
                at = taken[0]
                taken[0] += count * size
                return room[:, at:taken[0]].bitcast(dt)

            w_sb = share(KT * D, f32, 4).rearrange("p (t c) -> p t c", t=KT)
            big = share(2 * 2 * H * F1, f32, 4).rearrange("p (s k h f) -> p s k h f", s=2, k=2, h=H)
            s2_pair = share(H * 2 * MT, f32, 4).rearrange("p (h a m) -> p h a m", h=H, a=2)
            bd = share(2 * MT * H, f32, 4).rearrange("p (k m h) -> p k m h", k=2, m=MT)
            early = share(3 * H * QUADS, f16, 2)
            a_b = early[:, 0:4 * D].bitcast(f32).rearrange("p (a c) -> p a c", a=2)
            wa_prod = early[:, 4 * D:8 * D].bitcast(f32).rearrange("p (a c) -> p a c", a=2)
            vals = early.rearrange("p (s h q f) -> p s h q f", s=3, h=H, q=4)
            wa = sb("wa", [P, KT, 2 * H], f32)
            xt_sb = sb("xt_sb", [P, KT, N], f32)
            h_sb = sb("h_sb", [P, 2, D], f32)
            s_t = sb("s_t", [2 * H, 2, CHUNK], f32)
            s2_max = sb("s2_max", [P, H], f32)
            c_max = sb("c_max", [P, H], f32)
            BANKS = 6
            FIRST_LOADS = (2, 3, 6, 8, 10)
            EARLY = 4
            ps_s = ph.enter_context(nc.psum_tensor("ps_s", [P, 2, 512], f32))
            ps_h = ph.enter_context(nc.psum_tensor("ps_h", [P, BANKS, D], f32))
            ps_t = ps_h[:, EARLY:, :]

            w_loaded, a_loaded, x_loaded = sem("w_loaded"), sem("a_loaded"), [sem(f"x_loaded{c}") for c in range(CHUNKS)]
            id_zero, id_ready = sem("id_zero"), sem("id_ready")
            wa_prod_done, wa_ready = sem("wa_prod_done"), sem("wa_ready")
            s_done, s_col_ready = sem("s_done"), sem("s_col_ready")
            rows_stored = [sem(f"rows_stored{i}") for i in range(2)]
            s2_max_ready, c_max_ready, shifted, scaled_up = sem("s2_max_ready"), sem("c_max_ready"), sem("shifted"), sem("scaled_up")
            pairs_ready, exps_done = sem("pairs_ready"), sem("exps_done")
            st_done, st_ready = sem("st_done"), sem("st_ready")
            h_done, h_copied, pairs_stored = sem("h_done"), sem("h_copied"), sem("pairs_stored")
            big_ready, high_ready, low_ready = sem("big_ready"), sem("high_ready"), sem("low_ready")
            h_stored = [sem("h_stored0"), sem("h_stored1")]
            v_stored = [sem(f"v_stored{i}") for i in range(3)]

            block = ph.enter_context(nc.Block())

            @block.sync
            def _(sp):
                sp.dma_start(w_sb[:], w.rearrange("(t p) c -> p t c", p=P)).then_inc(w_loaded, 16)
                for a, src in enumerate((a1, a2)):
                    flat = src.rearrange("h f -> (h f)")[None, :]
                    sp.dma_start(a_b[:, a, :], flat.broadcast_to([P, D])).then_inc(a_loaded, 16)
                def load_x(c):
                    part = x_t[:, c * CHUNK:(c + 1) * CHUNK].rearrange("(t p) n -> p t n", p=P)
                    sp.dma_start(xt_sb[:, :, c * CHUNK:(c + 1) * CHUNK], part).then_inc(x_loaded[c], 16)

                def first_adj(c):
                    if c >= 2:
                        sp.wait_ge(adj_ready, c - 1)
                    load_adj(sp, 0, c, c % 2)

                AHEAD = 8
                for c in range(AHEAD):
                    load_x(c)
                for c in range(CHUNKS):
                    sp.wait_ge(st_ready, c + 1)
                    sp.dma_start(s_rows_dram[:, c * CHUNK:(c + 1) * CHUNK], s_t[:, c % 2, :]).then_inc(rows_stored[c % 2], 16)
                    if c + AHEAD < CHUNKS:
                        load_x(c + AHEAD)
                    if c in FIRST_LOADS:
                        first_adj(FIRST_LOADS.index(c))
                sp.wait_ge(pairs_ready, 2)
                sp.dma_start(s2_dram.rearrange("h p c -> p h c"),
                             s2_pair[:].rearrange("p h a m -> p h (a m)")).then_inc(pairs_stored, 16)
                for m in range(MT):
                    sp.wait_ge(h_copied, m + 1)
                    sp.dma_start(h_dram[m], h_sb[:, m % 2, :]).then_inc(h_stored[m % 2], 16)
                    sp.wait_ge(low_ready, 2 * (m + 1))
                    sp.dma_start(v_dram[:, :, m, :].rearrange("h p c -> p h c"),
                                 vals[:, m % 3].rearrange("p h q f -> p h (q f)")).then_inc(v_stored[m % 3], 16)
                    if m % 2 == 1 and m // 2 + 5 < ALOADS:
                        first_adj(m // 2 + 5)
                    if m == MT - 8:
                        for i in range(2):
                            sp.wait_ge(rows_stored[i], 16 * CHUNKS // 2)
                        sp.wait_ge(pairs_stored, 16)
                        load_row(sp, 0, 0, 0)
                for slot in range(2):
                    sp.wait_ge(h_stored[slot], 16 * MT // 2)
                for slot in range(3):
                    sp.wait_ge(v_stored[slot], 16 * MT // 3)

            @block.gpsimd
            def _(pool):
                nc.gpsimd.memset(ident[:], 0.0).then_inc(id_zero, 1)
                pool.wait_ge(id_zero, 1)
                nc.gpsimd.affine_select(out=ident[:], in_=ident[:], compare_op=ALU.not_equal, fill=1.0, base=0,
                                        pattern=[[-1, P]], channel_multiplier=1).then_inc(id_ready, 1)
                for c in range(ALOADS):
                    if c == 3:
                        pool.wait_ge(s2_max_ready, 1)
                        nc.gpsimd.partition_all_reduce(c_max[:], s2_max[:], P, RMAX).then_inc(c_max_ready, 1)
                    pool.wait_ge(adj_loaded[c % 2], 16 * (c // 2 + 1))
                    to_bytes(0, c)

            @block.vector
            def _(dve):
                dve.wait_ge(w_loaded, 16)
                dve.wait_ge(a_loaded, 32)
                for n in range(2 * KT):
                    a, k = n % 2, n // 2
                    if n >= 2:
                        dve.wait_ge(wa_ready, n - 1)
                    nc.vector.tensor_tensor(wa_prod[:, n % 2, :], w_sb[:, k, :], a_b[:, a, :],
                                            ALU.mult).then_inc(wa_prod_done, 1)
                    dve.wait_ge(wa_prod_done, n + 1)
                    nc.vector.tensor_reduce(wa[:, k, a * H:(a + 1) * H],
                                            wa_prod[:, n % 2, :].rearrange("p (h f) -> p h f", f=F),
                                            axis=AX.X, op=ALU.add).then_inc(wa_ready, 1)
                for half in range(2):
                    dve.wait_ge(s_done, CHUNKS // 2 * (half + 1))
                    nc.vector.tensor_copy(s_col[:, half * MT // 2:(half + 1) * MT // 2, :].rearrange("p m s -> p (m s)"),
                                          ps_s[:, half, 0:MT * H]).then_inc(s_col_ready, 1)
                dve.wait_ge(s_col_ready, 2)
                s1_hm = s_col[:, :, 0:H].rearrange("p m h -> p h m")
                s2_mh = s_col[:, :, H:2 * H]
                s2_hm = s2_mh.rearrange("p m h -> p h m")
                nc.vector.tensor_reduce(s2_max[:], s2_hm, axis=AX.X, op=ALU.max).then_inc(s2_max_ready, 1)
                nc.vector.tensor_copy(s2_pair[:, :, 0, :], s2_hm).then_inc(pairs_ready, 1)
                nc.vector.tensor_scalar_mul(s2_pair[:, :, 1, :], s2_hm, -1.0).then_inc(pairs_ready, 1)
                dve.wait_ge(c_max_ready, 1)
                c_mh = c_max[:][:, None, :].broadcast_to([P, MT, H])
                c_hm = c_max[:][:, :, None].broadcast_to([P, H, MT])
                nc.vector.tensor_tensor(bd[:, 0], s2_mh, c_mh, ALU.subtract).then_inc(shifted, 1)
                nc.vector.tensor_tensor(ratio[:], s1_hm, c_hm, ALU.add).then_inc(shifted, 1)
                dve.wait_ge(shifted, 2)
                nc.vector.tensor_scalar_min(ratio[:], ratio[:], 90.0).then_inc(shifted, 1)
                dve.wait_ge(exps_done, 3)
                nc.vector.tensor_scalar_mul(bd[:], bd[:], TOP * LOW).then_inc(scaled_up, 1)
                dve.wait_ge(scaled_up, 1)

                def low_parts(m):
                    dve.wait_ge(high_ready, m + 1)
                    for kind in range(2):
                        nc.vector.scalar_tensor_tensor(out=vals[:, m % 3, :, 2 * kind + 1, :],
                                                       in0=vals[:, m % 3, :, 2 * kind, :], scalar=-LOW,
                                                       in1=big[:, m % 2, kind], op0=ALU.mult,
                                                       op1=ALU.add).then_inc(low_ready, 1)

                for m in range(MT):
                    if m >= 2:
                        dve.wait_ge(low_ready, 2 * (m - 1))
                    dve.wait_ge(h_done, m + 1)
                    for kind in range(2):
                        factor = bd[:, kind, m, :][:, :, None].broadcast_to([P, H, F])
                        nc.vector.tensor_tensor(big[:, m % 2, kind, :, 0:F],
                                                ps_h[:, m % BANKS, :].rearrange("p (h f) -> p h f", f=F), factor,
                                                ALU.mult).then_inc(big_ready, 1)
                    nc.vector.tensor_copy(big[:, m % 2, :, :, F], bd[:, :, m, :]).then_inc(big_ready, 1)
                    if m >= 1:
                        low_parts(m - 1)
                low_parts(MT - 1)

            @block.tensor
            def _(pe):
                def turn(c):
                    pe.wait_ge(id_ready, 1)
                    pe.wait_ge(st_ready, c + 1)
                    for t in range(TPC):
                        at = ((c * TPC + t) % (MT // 2)) * 2 * H
                        last = nc.tensor.transpose(ps_s[:, c // (CHUNKS // 2), at:at + 2 * H],
                                                   s_t[:, c % 2, t * P:(t + 1) * P], ident[0:2 * H, 0:2 * H])
                    last.then_inc(s_done, 1)

                def h_tile(m):
                    for k in range(KT):
                        last = nc.tensor.matmul(ps_h[:, m % BANKS, :], xt_sb[:, k, m * P:(m + 1) * P], w_sb[:, k, :],
                                                start=k == 0, stop=k == KT - 1)
                    last.then_inc(h_done, 1)

                pe.wait_ge(w_loaded, 16)
                pe.wait_ge(x_loaded[0], 16)
                for m in range(EARLY):
                    h_tile(m)
                pe.wait_ge(wa_ready, 2 * KT)
                for c in range(CHUNKS):
                    pe.wait_ge(x_loaded[c], 16)
                    if c >= 2:
                        pe.wait_ge(st_ready, c - 1)
                    for k in range(KT):
                        last = nc.tensor.matmul(ps_t[0:2 * H, c % 2, :], wa[:, k, :],
                                                xt_sb[:, k, c * CHUNK:(c + 1) * CHUNK],
                                                start=k == 0, stop=k == KT - 1)
                    last.then_inc(st_done, 1)
                    if c >= 1:
                        turn(c - 1)
                turn(CHUNKS - 1)
                for m in range(EARLY, MT):
                    if m >= BANKS:
                        pe.wait_ge(h_copied, m - (BANKS - 1))
                        pe.wait_ge(big_ready, 3 * (m - (BANKS - 1)))
                    h_tile(m)

            @block.scalar
            def _(act):
                for c in range(CHUNKS):
                    act.wait_ge(st_done, c + 1)
                    if c >= 2:
                        act.wait_ge(s_done, c - 1)
                        act.wait_ge(rows_stored[c % 2], 16 * (c // 2))
                    nc.scalar.copy(s_t[:, c % 2, :], ps_t[0:2 * H, c % 2, :]).then_inc(st_ready, 1)
                act.wait_ge(shifted, 3)
                nc.scalar.activation(bd[:, 1], bd[:, 0], ACT.Exp, scale=SLOPE).then_inc(exps_done, 1)
                nc.scalar.activation(ratio[:], ratio[:], ACT.Exp, scale=1.0 - SLOPE).then_inc(exps_done, 1)
                act.wait_ge(exps_done, 1)
                nc.scalar.activation(bd[:, 0], bd[:, 0], ACT.Exp).then_inc(exps_done, 1)
                for m in range(MT):
                    act.wait_ge(big_ready, 3 * (m + 1))
                    if m >= 3:
                        act.wait_ge(v_stored[m % 3], 16 * (m // 3))
                    for kind in range(2):
                        last = nc.scalar.mul(vals[:, m % 3, :, 2 * kind, :], big[:, m % 2, kind], 1.0 / LOW)
                    last.then_inc(high_ready, 1)
                    if m >= 2:
                        act.wait_ge(h_stored[m % 2], 16 * (m // 2))
                    nc.scalar.copy(h_sb[:, m % 2, :], ps_h[:, m % BANKS, :]).then_inc(h_copied, 1)

        with ExitStack() as ph:
            def sb(name, shape, dt):
                return ph.enter_context(nc.sbuf_tensor("m_" + name, shape, dt))

            vals = sb("vals", [P, MT, QUADS], f16)
            sign = sb("sign", [P, SIGNS, G, BLOCK], i8)
            neg = sb("neg", [P, RING, G, BLOCK], u8)
            pos = sb("pos", [P, RING, G, BLOCK], u8)
            pos_sum = sb("pos_sum", [P, J, PAIR], f32)
            both = sb("both", [P, J, PAIR], f32)
            total = sb("total", [P, 2, J, F1], f32)
            att = sb("att", [P, J, D], f32)
            xz = sb("xz", [P, J, D], f32)
            ey = sb("ey", [P, J, D], f32)
            stats = sb("stats", [P, J, 6], f32)
            mv = sb("mv", [P, J, 2], f32)
            spread = sb("spread", [P, J], f32)
            rstd = sb("rstd", [P, J], f32)
            minus_half = sb("minus_half", [P, J], f32)
            minus_one = sb("minus_one", [P, J], f32)
            den = sb("den", [P, J], f32)
            rden = sb("rden", [P, J], f32)
            ok = sb("ok", [P, H, MT], f32)
            ok_v = sb("ok_v", [P, MT], f32)
            fails = sb("fails", [P, 2], f32)
            fail = sb("fail", [P, 1], f32)
            fail_all = sb("fail_all", [P, 1], f32)
            acc = ph.enter_context(nc.psum_tensor("acc", [P, 2, 4, 512], f32))

            v_loaded = [sem(f"v_loaded{k}") for k in range(VLOADS)]
            sign_act = sem("sign_act")
            sign_dve = sem("sign_dve")
            neg_ready = sem("neg_ready")
            masks_ready = sem("masks_ready")
            masks_used = sem("masks_used")
            pos_scaled = sem("pos_scaled")
            acc_free = sem("acc_free")
            both_ready, total_ready = sem("both_ready"), sem("total_ready")
            att_ready = sem("att_ready")
            x_in, pos_added, min_ready, exp_ready = sem("x_in"), sem("pos_added"), sem("min_ready"), sem("exp_ready")
            z_ready, stats_ready, var_ready, eps_added, pow_ready = sem("z_ready"), sem("stats_ready"), sem("var_ready"), sem("eps_added"), sem("pow_ready")
            y_ready, y_stored, consts = sem("y_ready"), sem("y_stored"), sem("consts")
            last_stored = [sem("last_stored0"), sem("last_stored1")]
            checked, fail_ready, fail_max = sem("checked"), sem("fail_ready"), sem("fail_max")
            flag_ready = sem("flag_ready")

            block = ph.enter_context(nc.Block())
            HEADS = BLOCKS * H
            HALVES = (slice(0, J // 2), slice(J // 2, J))
            LAST_PARTS = ((H - 1, slice(0, D - F)), (H, slice(D - F, D)))

            def row_tiles(dram, b):
                return dram[ds(b * BLOCK, BLOCK), :].rearrange("(j p) c -> p j c", p=P)

            @block.sync
            def _(sp):
                def load_values(h, k):
                    sp.dma_start(vals[:, k * VG:(k + 1) * VG, :],
                                 v_dram[ds(h, 1), :, k * VG:(k + 1) * VG, :]
                                 .rearrange("a p m c -> (a p) m c")).then_inc(v_loaded[k], 16)

                for k in range(VLOADS):
                    load_values(0, k)
                sp.dma_start(xz[:], row_tiles(x, 0)).then_inc(x_in, 16)
                sp.sem_inc(y_stored, 16)
                with sp.Fori(0, BLOCKS) as b:
                    with sp.Fori(0, H // 2) as hp:
                        for par in range(2):
                            n = sp.snap(b * H + hp * 2 + par)
                            for k in range(VLOADS):
                                sp.wait_ge(masks_used, n * GROUPS + (VG // G * (k + 1) + RING))
                                load_values((hp * 2 + (par + 1)) % H, k)
                                if k == 0 and par == 0:
                                    load_row(sp, b, hp * 2 + 1, 1)
                                if k == 0 and par == 1:
                                    with sp.If(n < HEADS - 1):
                                        load_row(sp, ((n + 1) // H) % BLOCKS, (hp * 2 + 2) % H, 0)
                                i = VLOADS * par + k
                                with sp.If((b < BLOCKS - 1) * (hp < ALOADS // (2 * VLOADS)) != 0):
                                    sp.wait_ge(adj_ready, (b + 1) * ALOADS + hp * (2 * VLOADS) + (i - 1))
                                    load_adj(sp, (b + 1) % BLOCKS, (hp * (2 * VLOADS) + i) % ALOADS, i % 2)
                                if k == 2 and par == 1:
                                    with sp.If((hp == 2) * (b > 0) != 0):
                                        sp.wait_ge(y_ready, b * J)
                                        sp.dma_start(row_tiles(out, (b + (BLOCKS - 1)) % BLOCKS), ey[:]).then_inc(y_stored, 16)
                                        sp.dma_start(xz[:], row_tiles(x, b)).then_inc(x_in, 16)
                for k in range(VLOADS):
                    sp.wait_ge(v_loaded[k], 16 * (HEADS + 1))
                last_rows = row_tiles(out, BLOCKS - 1)
                for half in range(2):
                    at = slice(half * J // 2, (half + 1) * J // 2)
                    sp.wait_ge(y_ready, (BLOCKS - 1) * J + (half + 1) * J // 2)
                    sp.dma_start(last_rows[:, at], ey[:, at]).then_inc(last_stored[half], 16)
                for half in range(2):
                    sp.wait_ge(last_stored[half], 16)
                sp.wait_ge(y_stored, 16 * BLOCKS)

            @block.gpsimd
            def _(pool):
                loads = [pool.alloc_register(f"adj_loads{slot}") for slot in range(2)]
                heads = pool.alloc_register("heads_up_to")
                stored = pool.alloc_register("stores_before")
                for slot in range(2):
                    pool.reg_mov(loads[slot], 8 * ALOADS + 16)
                pool.reg_mov(heads, H + 1)
                pool.reg_mov(stored, 2 * 16)

                def convert(par, c):
                    arrived = pool.snap(loads[c % 2])
                    pool.wait_ge(adj_loaded[c % 2], arrived)
                    pool.reg_add(loads[c % 2], loads[c % 2], 16)
                    to_bytes(par, c)

                def divide(b, h):
                    peeled = isinstance(b, int)
                    upto = b * H + h + 1 if peeled else pool.snap(heads)
                    at_block = b + 1 if peeled else pool.snap(b + 1)
                    pool.wait_ge(total_ready, upto)
                    pool.wait_ge(pos_added, at_block)
                    pool.wait_ge(min_ready, at_block)
                    if not peeled:
                        pool.reg_add(heads, heads, 1)
                    nc.gpsimd.tensor_scalar_max(den[:], total[:, h % 2, :, F], TINY)
                    pool.drain()
                    nc.gpsimd.tensor_tensor(rden[:], den[:], minus_one[:], ALU.pow)
                    pool.drain()
                    nc.gpsimd.tensor_tensor(att[:, :, h * F:(h + 1) * F], total[:, h % 2, :, 0:F],
                                            rden[:][:, :, None].broadcast_to([P, J, F]),
                                            ALU.mult).then_inc(att_ready, 1)

                def take_min(b):
                    pool.drain()
                    peeled = isinstance(b, int)
                    before = 16 * (b + 1) if peeled else pool.snap(stored)
                    pool.wait_ge(y_stored, before)
                    if not peeled:
                        pool.reg_add(stored, stored, 16)
                    nc.gpsimd.tensor_scalar_min(ey[:], att[:], 0.0).then_inc(min_ready, 1)

                def take_pow(b, part=0, rows=slice(0, J)):
                    pool.wait_ge(eps_added, b + (part + 1))
                    nc.gpsimd.tensor_tensor(rstd[:, rows], spread[:, rows], minus_half[:, rows],
                                            ALU.pow).then_inc(pow_ready, 1)

                nc.gpsimd.memset(minus_half[:], -0.5).then_inc(consts, 1)
                nc.gpsimd.memset(minus_one[:], -1.0).then_inc(consts, 1)
                pool.wait_ge(consts, 2)
                pool.sem_inc(min_ready, 1)
                pool.sem_inc(att_ready, 2)

                def work_through(b, par=None, first=False):
                    for h in range(H):
                        for k in range(VLOADS):
                            if h == 3 and k == 2 and not first:
                                take_pow(b - 1)
                            if par is not None and h * VLOADS + k < ALOADS:
                                convert(par, h * VLOADS + k)
                        divide(b, h)

                work_through(0, 1, first=True)
                take_min(0)
                with pool.Fori(0, (BLOCKS - 2) // 2) as i:
                    for par in range(2):
                        b = pool.snap(i * 2 + (1 + par))
                        work_through(b, par)
                        take_min(b)
                work_through(BLOCKS - 1)
                for half, rows in enumerate(HALVES):
                    take_pow(BLOCKS - 1, half, rows)
                pool.wait_ge(fail_ready, 1)
                nc.gpsimd.partition_all_reduce(fail_all[:], fail[:], P, RMAX).then_inc(fail_max, 1)

            @block.scalar
            def _(act):
                def scale_pos(m, par):
                    act.wait_ge(masks_used, m * GROUPS + (GROUPS + RING))
                    act.wait_ge(acc_free, m + 2)
                    for j in range(J):
                        row = ratio[:, ds(m % H, 1), ds((m // H) * J + j, 1)].rearrange("p a b -> p (a b)")
                        last = nc.scalar.activation(pos_sum[:, j, :],
                                                    acc[:, par, j // 3, (j % 3) * PAIR:(j % 3 + 1) * PAIR],
                                                    ACT.Identity, scale=row)
                    last.then_inc(pos_scaled, 1)

                def take_exp(b, part=0, cols=slice(0, D)):
                    act.wait_ge(min_ready, b + (part + 2))
                    nc.scalar.activation(ey[:, :, cols], ey[:, :, cols], ACT.Exp).then_inc(exp_ready, 1)

                with act.Fori(0, BLOCKS) as b:
                    with act.Fori(0, H // 2) as hp:
                        for par in range(2):
                            n = act.snap(b * H + hp * 2 + par)
                            first = act.snap(n * GROUPS)
                            act.wait_ge(row_loaded[par], (b * (H // 2) + hp) * 32 + 32)
                            for g in range(GROUPS):
                                act.wait_ge(neg_ready, first + (g + 1))
                                for t in range(DVE_TILES[g], G):
                                    m = g * G + t
                                    last = nc.scalar.activation(sign[:, g % SIGNS, t, :], s1_b[:, par, :], ACT.Sign,
                                                                bias=s2_c[:, par, 0, m:m + 1])
                                last.then_inc(sign_act, 1)
                                if g == AT_SCALE and par == 1:
                                    scale_pos(n - 1, 0)
                                if g == AT_SCALE and par == 0:
                                    with act.If(n > 0):
                                        scale_pos((n + (HEADS - 1)) % HEADS, 1)
                                if g == GROUPS - 1 and par == 0:
                                    with act.If((hp == 0) * (b > 0) != 0):
                                        take_exp((b + (BLOCKS - 1)) % BLOCKS)
                for part, (_, cols) in enumerate(LAST_PARTS):
                    if part == 1:
                        scale_pos(HEADS - 1, 1)
                    take_exp(BLOCKS - 1, part, cols)

            @block.vector
            def _(dve):
                def signs(par, g):
                    for t in range(DVE_TILES[g]):
                        m = g * G + t
                        last = nc.vector.tensor_scalar(sign[:, g % SIGNS, t, :].bitcast(u8), s1_b[:, par, :],
                                                       s2_c[:, par, 1, m:m + 1], 128.0, ALU.is_lt, ALU.mult)
                    last.then_inc(sign_dve, 1)

                def gather(m, par):
                    dve.wait_ge(pos_scaled, m + 1)
                    for half in range(2):
                        nc.vector.tensor_tensor(both[:, 3 * half:3 * half + 3, :].rearrange("p j c -> p (j c)"),
                                                acc[:, par, 2 + half, 0:3 * PAIR],
                                                pos_sum[:, 3 * half:3 * half + 3, :].rearrange("p j c -> p (j c)"),
                                                ALU.add).then_inc(both_ready if half == 0 else acc_free, 1)
                    dve.wait_ge(both_ready, m + 1)
                    dve.wait_ge(acc_free, m + 3)
                    dve.wait_ge(att_ready, m + 1)
                    nc.vector.scalar_tensor_tensor(out=total[:, par], in0=both[:, :, F1:PAIR], scalar=1.0 / LOW,
                                                   in1=both[:, :, 0:F1], op0=ALU.mult,
                                                   op1=ALU.add).then_inc(total_ready, 1)
                    dve.wait_ge(total_ready, m + 1)
                    nc.vector.tensor_copy(dens[:, ds(m % H, 1), ds((m // H) * J, J)], total[:, par, :, F][:, None, :])

                def add_positive(b, heads=H, cols=slice(0, D)):
                    dve.wait_ge(att_ready, b * H + (heads + 2))
                    dve.wait_ge(x_in, b * 16 + 16)
                    nc.vector.scalar_tensor_tensor(out=xz[:, :, cols], in0=att[:, :, cols], scalar=0.0,
                                                   in1=xz[:, :, cols], op0=ALU.max, op1=ALU.add).then_inc(pos_added, 1)

                def add_negative(b, part=0, cols=slice(0, D)):
                    dve.wait_ge(pos_added, b + (part + 2))
                    dve.wait_ge(exp_ready, b + (part + 1))
                    nc.vector.scalar_tensor_tensor(out=xz[:, :, cols], in0=ey[:, :, cols], scalar=-1.0,
                                                   in1=xz[:, :, cols], op0=ALU.add, op1=ALU.add).then_inc(z_ready, 1)

                def row_stats(b, half):
                    dve.wait_ge(z_ready, b + 1)
                    for j in range(J)[HALVES[half]]:
                        nc.vector.bn_stats(stats[:, j, :], xz[:, j, :])
                    dve.drain()
                    for j in range(J)[HALVES[half]]:
                        last = nc.vector.bn_aggr(mv[:, j, :], stats[:, j, :])
                    last.then_inc(var_ready, 1)

                def add_eps(b, halves, rows=slice(0, J)):
                    dve.wait_ge(var_ready, b * 2 + halves)
                    nc.vector.tensor_scalar_add(spread[:, rows], mv[:, rows, 1], EPS).then_inc(eps_added, 1)

                def keep_moments(b):
                    nc.vector.tensor_copy(moments[:, ds(b * J, J), :], mv[:])

                def normalise(b, half, part=0):
                    dve.wait_ge(pow_ready, b + (part + 1))
                    for j in range(J)[HALVES[half]]:
                        nc.vector.tensor_scalar(ey[:, j, :], xz[:, j, :], mv[:, j, 0:1], rstd[:, j:j + 1],
                                                ALU.subtract, ALU.mult).then_inc(y_ready, 1)

                def end_stats(b):
                    row_stats(b, 1)
                    add_eps(b, 2)
                    keep_moments(b)

                dve.sem_inc(neg_ready, SIGNS)
                dve.sem_inc(acc_free, 2)
                dve.sem_inc(pos_added, 1)
                with dve.Fori(0, BLOCKS) as b:
                    b_par = dve.snap(b % 2)
                    with dve.Fori(0, H // 2) as hp:
                        for par in range(2):
                            n = dve.snap(b * H + hp * 2 + par)
                            first = dve.snap(n * GROUPS)
                            if par == 0:
                                dve.wait_ge(adj_ready, b * ALOADS + ALOADS)
                            dve.wait_ge(row_loaded[par], (b * (H // 2) + hp) * 32 + 32)
                            signs(par, 0)
                            for g in range(GROUPS):
                                words = [t[:, g % ring].rearrange("p t n -> p (t n)").bitcast(u32)
                                         for t, ring in ((sign, SIGNS), (neg, RING), (pos, RING))]
                                near = adj_one[:, ds(b_par, 1), g * G:(g + 1) * G, :] \
                                    .rearrange("p a t n -> p (a t n)").bitcast(u32)
                                dve.wait_ge(masks_used, first + (g + 1))
                                dve.wait_ge(sign_dve, first + (g + 1))
                                dve.wait_ge(sign_act, first + (g + 1))
                                nc.vector.scalar_tensor_tensor(out=words[1], in0=words[0], scalar=4, in1=near,
                                                               op0=ALU.logical_shift_right,
                                                               op1=ALU.bitwise_and).then_inc(neg_ready, 1)
                                if g < GROUPS - 1:
                                    signs(par, g + 1)
                                dve.wait_ge(neg_ready, first + (g + 1 + SIGNS))
                                nc.vector.tensor_tensor(words[2], words[1], near, ALU.bitwise_xor) \
                                    .then_inc(masks_ready, 1)
                                if g == AT_GATHER and par == 1:
                                    gather(n - 1, 0)
                                if g == AT_GATHER and par == 0:
                                    with dve.If(n > 0):
                                        gather((n + (HEADS - 1)) % HEADS, 1)
                                before = (b + (BLOCKS - 1)) % BLOCKS
                                pieces = {0: (lambda: add_positive(before), lambda: row_stats(before, 0),
                                              lambda: normalise(before, 0)),
                                          1: (lambda: add_negative(before), lambda: end_stats(before),
                                              lambda: normalise(before, 1))}[par]
                                for at_pair, piece in enumerate(pieces):
                                    if g == (AT_ADD if par == 0 and at_pair == 0 else 2 + at_pair):
                                        with dve.If((hp == at_pair) * (b > 0) != 0):
                                            piece()
                last_block = BLOCKS - 1
                for part, (heads, cols) in enumerate(LAST_PARTS):
                    if part == 1:
                        gather(HEADS - 1, 1)
                        nc.vector.tensor_scalar(ok[:], ratio[:], 1.0, FLOOR, ALU.add, ALU.mult).then_inc(checked, 1)
                        dve.wait_ge(checked, 1)
                        nc.vector.tensor_tensor(ok[:], dens[:], ok[:], ALU.is_ge).then_inc(checked, 1)
                        dve.wait_ge(checked, 2)
                        nc.vector.scalar_tensor_tensor(out=ok[:], in0=ratio[:], scalar=HUGE, in1=ok[:], op0=ALU.is_le,
                                                       op1=ALU.mult).then_inc(checked, 1)
                    dve.wait_ge(att_ready, last_block * H + (heads + 2))
                    dve.wait_ge(y_stored, 16 * BLOCKS)
                    nc.vector.tensor_scalar_min(ey[:, :, cols], att[:, :, cols], 0.0).then_inc(min_ready, 1)
                    add_positive(last_block, heads, cols)
                    add_negative(last_block, part, cols)
                dve.wait_ge(z_ready, BLOCKS + 1)
                for half, rows in enumerate(HALVES):
                    row_stats(last_block, half)
                    add_eps(last_block, half + 1, rows)
                for half in range(2):
                    normalise(last_block, half, half)
                keep_moments(last_block)
                dve.drain()
                nc.vector.tensor_scalar(ok_v[:], moments[:, :, 1], HUGE, None, ALU.is_le).then_inc(checked, 1)
                dve.wait_ge(checked, 4)
                nc.vector.tensor_reduce(fails[:, 0:1], ok[:].rearrange("p h m -> p (h m)"), axis=AX.X,
                                        op=ALU.min).then_inc(checked, 1)
                nc.vector.tensor_reduce(fails[:, 1:2], ok_v[:], axis=AX.X, op=ALU.min).then_inc(checked, 1)
                dve.wait_ge(checked, 6)
                nc.vector.tensor_tensor(fail[:], fails[:, 0:1], fails[:, 1:2], ALU.min).then_inc(checked, 1)
                dve.wait_ge(checked, 7)
                nc.vector.tensor_scalar(fail[:], fail[:], -1.0, 1.0, ALU.mult, ALU.add).then_inc(fail_ready, 1)
                dve.wait_ge(fail_max, 1)
                nc.vector.tensor_copy(flag[:], fail_all[:]).then_inc(flag_ready, 1)

            @block.tensor
            def _(pe):
                pe.sem_inc(masks_used, RING)
                count = pe.alloc_register("group_count")
                pe.reg_mov(count, 1)
                with pe.Fori(0, HEADS // 2) as i:
                    for par in range(2):
                        for g in range(GROUPS):
                            upto = pe.snap(count)
                            if g == 0:
                                pe.wait_ge(acc_free, i * 2 + (par + 1))
                            if g * G % VG == 0:
                                pe.wait_ge(v_loaded[g * G // VG], i * 32 + 16 * (par + 1))
                            pe.wait_ge(masks_ready, upto)
                            pe.reg_add(count, count, 1)
                            for t in range(G):
                                m = g * G + t
                                for j in range(J):
                                    for side, mask in enumerate((pos, neg)):
                                        last = nc.tensor.matmul(
                                            acc[:, par, 2 * side + j // 3, (j % 3) * PAIR:(j % 3 + 1) * PAIR],
                                            mask[:, g % RING, t, j * P:(j + 1) * P].bitcast(f8),
                                            vals[:, m, side * PAIR:(side + 1) * PAIR],
                                            start=m == 0 and j % 3 == 0, stop=m == MT - 1,
                                            skip_group_check=True)
                            last.then_inc(masks_used, 1)

        edges.close()

        with ExitStack() as ph:
            def sb(name, shape, dt):
                return ph.enter_context(nc.sbuf_tensor("g_" + name, shape, dt))

            adj_row = sb("adj_row", [P, N], i32)
            mask = sb("mask", [P, N], f32)
            s2_b = sb("s2_b", [P, N], f32)
            score = sb("score", [P, N], f32)
            e_t = sb("e_t", [P, MT, P], f32)
            h_head = sb("h_head", [P, MT, F], f32)
            x_row = sb("x_row", [P, D], f32)
            att = sb("att", [P, D], f32)
            elu_n = sb("elu_n", [P, D], f32)
            y_row = sb("y_row", [P, D], f32)
            neg_max = sb("neg_max", [P, 1], f32)
            den = sb("den", [P, 1], f32)
            rden = sb("rden", [P, 1], f32)
            stats = sb("stats", [P, 6], f32)
            mv = sb("mv", [P, 2], f32)
            rstd = sb("rstd", [P, 1], f32)
            expo = sb("expo", [P, 1], f32)
            neg_off = adj_row[:].bitcast(f32)
            scaled = e_t[:].rearrange("p m n -> p (m n)")
            ps_e = ph.enter_context(nc.psum_tensor("ps_e", [P, 2, 4 * P], f32))
            ps_o = ph.enter_context(nc.psum_tensor("ps_o", [P, 512], f32))
            TG = MT // 4

            g_adj, g_x, g_s2, g_h = sem("g_adj"), sem("g_x"), sem("g_s2"), sem("g_h")
            g_mask, g_off = sem("g_mask"), sem("g_off")
            g_dve, g_exp, g_tr, g_trc, g_pv = sem("g_dve"), sem("g_exp"), sem("g_tr"), sem("g_trc"), sem("g_pv")
            g_tail, g_elu, g_pow, g_y, g_out = sem("g_tail"), sem("g_elu"), sem("g_pow"), sem("g_y"), sem("g_out")
            g_ex, g_free = sem("g_ex"), sem("g_free")
            block = ph.enter_context(nc.Block())
            STEPS = 5
            TAIL = 6

            @block.sync
            def _(sp):
                redo = sp.value_load(flag[0:1, 0:1])
                with sp.If(redo != 0):
                    sp.sem_inc(g_free, 1)
                    sp.sem_inc(g_out, 16)
                    with sp.Fori(0, MT) as i:
                        sp.dma_start(adj_row[:], adj[ds(i * P, P), :]).then_inc(g_adj, 16)
                        sp.dma_start(x_row[:], x[ds(i * P, P), :]).then_inc(g_x, 16)
                        with sp.Fori(0, H) as h:
                            sp.wait_ge(g_free, i * H + h + 1)
                            sp.dma_start(s2_b[:], s_rows_dram[ds(h + H, 1), :].broadcast_to([P, N])).then_inc(g_s2, 16)
                            sp.dma_start(h_head[:], h_dram.rearrange("m p (h f) -> h p m f", f=F)[ds(h, 1)]
                                         .rearrange("a p m f -> (a p) m f")).then_inc(g_h, 16)
                        sp.wait_ge(g_y, i + 1)
                        sp.dma_start(out[ds(i * P, P), :], y_row[:]).then_inc(g_out, 16)
                    sp.wait_ge(g_out, 16 * MT + 16)

            @block.vector
            def _(dve):
                redo = dve.value_load(flag[0:1, 0:1])
                with dve.If(redo != 0):
                    with dve.Fori(0, MT) as i:
                        dve.wait_ge(g_adj, i * 16 + 16)
                        nc.vector.tensor_scalar(mask[:], adj_row[:], 0.0, None, ALU.is_gt).then_inc(g_mask, 1)
                        dve.wait_ge(g_mask, i + 1)
                        nc.vector.tensor_scalar(neg_off, mask[:], -1.0, NEG_BIG, ALU.add, ALU.mult).then_inc(g_off, 1)
                        with dve.Fori(0, H) as h:
                            n = dve.snap(i * H + h)
                            base = dve.snap(n * STEPS)
                            s1 = s_col[:, ds(i, 1), ds(h, 1)].rearrange("p a b -> p (a b)")
                            dve.wait_ge(g_s2, n * 16 + 16)
                            nc.vector.tensor_scalar(scaled, s2_b[:], s1, SLOPE, ALU.add, ALU.mult).then_inc(g_dve, 1)
                            dve.wait_ge(g_dve, base + 1)
                            nc.vector.scalar_tensor_tensor(out=score[:], in0=s2_b[:], scalar=s1, in1=scaled,
                                                           op0=ALU.add, op1=ALU.max).then_inc(g_dve, 1)
                            dve.wait_ge(g_dve, base + 2)
                            nc.vector.tensor_tensor(score[:], score[:], mask[:], ALU.mult).then_inc(g_dve, 1)
                            dve.wait_ge(g_off, i + 1)
                            dve.wait_ge(g_dve, base + 3)
                            nc.vector.tensor_tensor(score[:], score[:], neg_off, ALU.add).then_inc(g_dve, 1)
                            dve.wait_ge(g_dve, base + 4)
                            nc.vector.tensor_reduce(neg_max[:], score[:], axis=AX.X, op=ALU.max, negate=True).then_inc(g_dve, 1)
                            dve.wait_ge(g_exp, n + 1)
                            nc.vector.reciprocal(rden[:], den[:]).then_inc(g_ex, 1)
                            dve.wait_ge(g_ex, n + 1)
                            dve.wait_ge(g_pv, n + 1)
                            nc.vector.tensor_scalar(att[:, ds(h * F, F)], ps_o[:, 0:F], rden[:], None,
                                                    ALU.mult).then_inc(g_free, 1)
                        tail = dve.snap(i * TAIL)
                        dve.wait_ge(g_free, i * H + H + 1)
                        nc.vector.tensor_scalar_min(elu_n[:], att[:], 0.0).then_inc(g_tail, 1)
                        dve.wait_ge(g_elu, i + 1)
                        dve.wait_ge(g_x, i * 16 + 16)
                        nc.vector.scalar_tensor_tensor(out=elu_n[:], in0=elu_n[:], scalar=-1.0, in1=x_row[:],
                                                       op0=ALU.add, op1=ALU.add).then_inc(g_tail, 1)
                        dve.wait_ge(g_tail, tail + 2)
                        nc.vector.scalar_tensor_tensor(out=att[:], in0=att[:], scalar=0.0, in1=elu_n[:],
                                                       op0=ALU.max, op1=ALU.add).then_inc(g_tail, 1)
                        dve.wait_ge(g_tail, tail + 3)
                        nc.vector.bn_stats(stats[:], att[:]).then_inc(g_tail, 1)
                        dve.drain()
                        nc.vector.bn_aggr(mv[:], stats[:]).then_inc(g_tail, 1)
                        dve.wait_ge(g_tail, tail + 5)
                        nc.vector.tensor_scalar_add(mv[:, 1:2], mv[:, 1:2], EPS).then_inc(g_tail, 1)
                        dve.wait_ge(g_out, i * 16 + 16)
                        dve.wait_ge(g_pow, i + 2)
                        nc.vector.tensor_scalar(y_row[:], att[:], mv[:, 0:1], rstd[:], ALU.subtract,
                                                ALU.mult).then_inc(g_y, 1)

            @block.gpsimd
            def _(pool):
                redo = pool.value_load(flag[0:1, 0:1])
                with pool.If(redo != 0):
                    nc.gpsimd.memset(expo[:], -0.5).then_inc(g_pow, 1)
                    pool.wait_ge(g_pow, 1)
                    with pool.Fori(0, MT) as i:
                        pool.wait_ge(g_tail, i * TAIL + TAIL)
                        nc.gpsimd.tensor_tensor(rstd[:], mv[:, 1:2], expo[:], ALU.pow).then_inc(g_pow, 1)

            @block.scalar
            def _(act):
                redo = act.value_load(flag[0:1, 0:1])
                with act.If(redo != 0):
                    with act.Fori(0, MT) as i:
                        with act.Fori(0, H) as h:
                            n = act.snap(i * H + h)
                            act.wait_ge(g_dve, n * STEPS + STEPS)
                            nc.scalar.activation(score[:], score[:], ACT.Exp, bias=neg_max[:],
                                                 accum_out=den[:]).then_inc(g_exp, 1)
                            for g in range(TG):
                                act.wait_ge(g_tr, n * TG + (g + 1))
                                nc.scalar.copy(e_t[:, g * 4:(g + 1) * 4, :].rearrange("p a b -> p (a b)"),
                                               ps_e[:, g % 2, :]).then_inc(g_trc, 1)
                        act.wait_ge(g_tail, i * TAIL + 1)
                        nc.scalar.activation(elu_n[:], elu_n[:], ACT.Exp).then_inc(g_elu, 1)

            @block.tensor
            def _(pe):
                redo = pe.value_load(flag[0:1, 0:1])
                with pe.If(redo != 0):
                    with pe.Fori(0, MT) as i:
                        with pe.Fori(0, H) as h:
                            n = pe.snap(i * H + h)
                            pe.wait_ge(g_exp, n + 1)
                            for g in range(TG):
                                if g >= 2:
                                    pe.wait_ge(g_trc, n * TG + (g - 1))
                                for t in range(4):
                                    m = g * 4 + t
                                    last = nc.tensor.transpose(ps_e[:, g % 2, t * P:(t + 1) * P],
                                                               score[:, m * P:(m + 1) * P], ident[:])
                                last.then_inc(g_tr, 1)
                            pe.wait_ge(g_trc, n * TG + TG)
                            pe.wait_ge(g_h, n * 16 + 16)
                            pe.wait_ge(g_free, n + 1)
                            for m in range(MT):
                                last = nc.tensor.matmul(ps_o[:, 0:F], e_t[:, m, :], h_head[:, m, :],
                                                        start=m == 0, stop=m == MT - 1)
                            last.then_inc(g_pv, 1)


def kernel(x, adj, L0_gnn_W, L0_gnn_a1, L0_gnn_a2):
    import numpy as np
    import concourse.bacc as bacc
    from concourse import mybir
    from concourse.bass_utils import run_bass_kernel_spmd

    nc = bacc.Bacc("TRN2", target_bir_lowering=False, num_devices=1)
    x, adj, w = np.asarray(x), np.asarray(adj), np.asarray(L0_gnn_W)
    layouts = {
        "x": x, "x_t": x.T, "adj": adj, "adj_t": adj.T,
        "w": w.transpose(1, 0, 2).reshape(w.shape[1], -1),
        "a1": np.asarray(L0_gnn_a1), "a2": np.asarray(L0_gnn_a2),
    }
    arrays, args = {}, []
    for name, a in layouts.items():
        a = np.ascontiguousarray(a)
        arrays[f"in_{name}"] = a
        args.append(nc.dram_tensor(f"in_{name}", a.shape, mybir.dt.from_np(a.dtype), kind="ExternalInput").ap())
    args.append(nc.dram_tensor("out_y", x.shape, mybir.dt.float32, kind="ExternalOutput").ap())
    build(nc, *args)
    r = run_bass_kernel_spmd(nc, [arrays], core_ids=[0])
    return r.results[0]["out_y"]
```
